# Optimizing a Trainium2 kernel written in Bass

```python
import numpy as np
import jax
import jax.numpy as jnp

def _softmax(x, axis=-1):
    return jax.nn.softmax(x, axis=axis)

def _gelu(x):
    return jax.nn.gelu(x, approximate=True)

def _silu(x):
    return jax.nn.silu(x)

def _sigmoid(x):
    return jax.nn.sigmoid(x)

def _layernorm(x, axis=-1, eps=1e-05):
    m = jnp.mean(x, axis=axis, keepdims=True)
    v = jnp.var(x, axis=axis, keepdims=True)
    return (x - m) / jnp.sqrt(v + eps)

def _scatter_add(tgt, idx, src, axis=0):
    return tgt.at[idx].add(src)

def _segment_sum(src, seg, n):
    return jax.ops.segment_sum(src, seg, n)
kernel_name = 'mk_gnn_ffn_d2_gnn_r16_b091b0'

def setup_inputs(seed: int=0):
    np.random.seed(seed)
    _w = jnp.asarray

    def _rec_inputs():
        import jax
        import jax.numpy as jnp
        _gk = jax.random.key(seed)
        x = -0.0002117 + 1 * jax.random.normal(jax.random.fold_in(_gk, 1), (6250, 256), jnp.float32)
        src = jax.random.randint(jax.random.fold_in(_gk, 2), (100000,), 0, 6250, jnp.int32)
        dst = jnp.minimum((6250 * jax.random.uniform(jax.random.fold_in(_gk, 3), (100000,)) ** 2.0).astype(jnp.int32), 99999)
        _o = jnp.argsort(dst, stable=True)
        src = src[_o]
        dst = dst[_o]
        edge_type_16 = jax.random.randint(jax.random.fold_in(_gk, 12), (100000,), 0, 16, jnp.int32)
        edge_weight = jax.random.uniform(jax.random.fold_in(_gk, 13), (100000,), jnp.float32, 0.0, 1)
        edge_weight1 = jax.random.uniform(jax.random.fold_in(_gk, 14), (100000, 1), jnp.float32, 0.0, 1)
        return (x, src, dst, edge_type_16, edge_weight, edge_weight1)
    x, src, dst, edge_type_16, edge_weight, edge_weight1 = _rec_inputs()

    def _L0_gnn_setup():
        import jax, jax.numpy as jnp
        import numpy as np
        N_NODES = 6250
        N_EDGES = 200000
        IN_FEATS = 256
        OUT_FEATS = 256
        key = jax.random.key(seed)
        k1, k2, k3, k4, k5, k6 = jax.random.split(key, 6)
        features = jax.random.normal(k1, (N_NODES, IN_FEATS), dtype=jnp.float32)
        edge_src = jax.random.randint(k2, (N_EDGES,), 0, N_NODES, dtype=jnp.int64)
        edge_dst = jnp.sort(jax.random.randint(k3, (N_EDGES,), 0, N_NODES, dtype=jnp.int64))
        edge_weight = jax.random.uniform(k4, (N_EDGES,), dtype=jnp.float32)
        bound = 1.0 / np.sqrt(IN_FEATS)
        W = jax.random.uniform(k5, (OUT_FEATS, IN_FEATS), dtype=jnp.float32, minval=-bound, maxval=bound)
        b = jax.random.uniform(k6, (OUT_FEATS,), dtype=jnp.float32, minval=-bound, maxval=bound)
        return {'features': features, 'edge_src': edge_src, 'edge_dst': edge_dst, 'edge_weight': edge_weight, 'W': W, 'b': b}
    _L0_gnn_all = _L0_gnn_setup()
    _L0_gnn_in = {k: v for k, v in _L0_gnn_all.items() if k in ('W', 'b')}
    del _L0_gnn_all

    def _L0_ffn_setup():
        import jax, jax.numpy as jnp
        import numpy as np
        B, S, D = (8, 256, 256)
        H = 4 * D
        CAPACITY = 0.5
        key = jax.random.key(seed)
        ks = jax.random.split(key, 6)
        x = jax.random.normal(ks[0], (B, S, D), dtype=jnp.float32)
        attention_mask = jnp.zeros((B, 1, 1, S), dtype=jnp.float32)
        wr = jax.random.normal(ks[1], (D, 1), dtype=jnp.float32) * 0.02
        br = jnp.zeros((1,), dtype=jnp.float32)
        w1 = jax.random.normal(ks[2], (D, H), dtype=jnp.float32) * 0.02
        b1 = jnp.zeros((H,), dtype=jnp.float32)
        w2 = jax.random.normal(ks[3], (H, D), dtype=jnp.float32) * 0.02
        b2 = jnp.zeros((D,), dtype=jnp.float32)
        return {'x': x, 'attention_mask': attention_mask, 'wr': wr, 'br': br, 'w1': w1, 'b1': b1, 'w2': w2, 'b2': b2}
    _L0_ffn_all = _L0_ffn_setup()
    _L0_ffn_in = {k: v for k, v in _L0_ffn_all.items() if k in ('attention_mask', 'wr', 'br', 'w1', 'b1', 'w2', 'b2')}
    del _L0_ffn_all

    def _L1_gnn_setup():
        import jax, jax.numpy as jnp
        import numpy as np
        N_NODES = 3125
        N_EDGES = 50000
        NUM_RELS = 16
        FEAT = 256
        OUT = 256
        key = jax.random.key(seed)
        ks = jax.random.split(key, 7)
        h = jax.random.normal(ks[0], (N_NODES, FEAT), dtype=jnp.float32)
        norm = jax.random.uniform(ks[1], (N_EDGES, 1), dtype=jnp.float32)
        weight = jax.random.normal(ks[2], (NUM_RELS, FEAT, OUT), dtype=jnp.float32) * 0.05
        gate_weight = jax.random.normal(ks[3], (NUM_RELS, FEAT, 1), dtype=jnp.float32) * 0.05
        src = jax.random.randint(ks[4], (N_EDGES,), 0, N_NODES)
        dst = jax.random.randint(ks[5], (N_EDGES,), 0, N_NODES)
        rel_type = jax.random.randint(ks[6], (N_EDGES,), 0, NUM_RELS)
        return {'h': h, 'norm': norm, 'weight': weight, 'gate_weight': gate_weight, 'src': src, 'dst': dst, 'rel_type': rel_type}
    _L1_gnn_all = _L1_gnn_setup()
    _L1_gnn_in = {k: v for k, v in _L1_gnn_all.items() if k in ('weight', 'gate_weight')}
    del _L1_gnn_all

    def _L1_ffn_setup():
        import jax, jax.numpy as jnp
        import numpy as np
        TOP_K = 2
        key = jax.random.key(seed)
        ks = jax.random.split(key, 4)
        B, L, D, H, E = (8, 256, 256, 1024, 8)
        s = 0.02
        return {'x': jax.random.normal(ks[0], (B, L, D), jnp.float32), 'Wg': jax.random.normal(ks[1], (D, E), jnp.float32) * s, 'bg': jnp.zeros((E,), jnp.float32), 'W1': jax.random.normal(ks[2], (E, D, H), jnp.float32) * s, 'b1': jnp.zeros((E, H), jnp.float32), 'W2': jax.random.normal(ks[3], (E, H, D), jnp.float32) * s, 'b2': jnp.zeros((E, D), jnp.float32)}
    _L1_ffn_all = _L1_ffn_setup()
    _L1_ffn_in = {k: v for k, v in _L1_ffn_all.items() if k in ('Wg', 'bg', 'W1', 'b1', 'W2', 'b2')}
    del _L1_ffn_all
    return {'x': x, 'src': src, 'dst': dst, 'edge_type_16': edge_type_16, 'edge_weight': edge_weight, 'edge_weight1': edge_weight1, 'L0_gnn_W': _L0_gnn_in['W'], 'L0_gnn_b': _L0_gnn_in['b'], 'L0_ffn_attention_mask': _L0_ffn_in['attention_mask'], 'L0_ffn_wr': _L0_ffn_in['wr'], 'L0_ffn_br': _L0_ffn_in['br'], 'L0_ffn_w1': _L0_ffn_in['w1'], 'L0_ffn_b1': _L0_ffn_in['b1'], 'L0_ffn_w2': _L0_ffn_in['w2'], 'L0_ffn_b2': _L0_ffn_in['b2'], 'L1_gnn_weight': _L1_gnn_in['weight'], 'L1_gnn_gate_weight': _L1_gnn_in['gate_weight'], 'L1_ffn_Wg': _L1_ffn_in['Wg'], 'L1_ffn_bg': _L1_ffn_in['bg'], 'L1_ffn_W1': _L1_ffn_in['W1'], 'L1_ffn_b1': _L1_ffn_in['b1'], 'L1_ffn_W2': _L1_ffn_in['W2'], 'L1_ffn_b2': _L1_ffn_in['b2']}

def reference(x, src, dst, edge_type_16, edge_weight, edge_weight1, L0_gnn_W, L0_gnn_b, L0_ffn_attention_mask, L0_ffn_wr, L0_ffn_br, L0_ffn_w1, L0_ffn_b1, L0_ffn_w2, L0_ffn_b2, L1_gnn_weight, L1_gnn_gate_weight, L1_ffn_Wg, L1_ffn_bg, L1_ffn_W1, L1_ffn_b1, L1_ffn_W2, L1_ffn_b2):
    import jax
    import jax.numpy as jnp

    def _L0_gnn_ref(features, edge_src, edge_dst, edge_weight, W, b):
        import jax, jax.numpy as jnp
        import numpy as np
        N_NODES = 6250
        N_EDGES = 200000
        IN_FEATS = 256
        OUT_FEATS = 256
        msgs = features[edge_src] * edge_weight[:, None]
        agg = jax.ops.segment_sum(msgs, edge_dst, num_segments=N_NODES, indices_are_sorted=True)
        return jnp.einsum('ni,oi->no', agg, W) + b

    def _L0_ffn_ref(x, attention_mask, wr, br, w1, b1, w2, b2):
        import jax, jax.numpy as jnp
        import numpy as np
        B, S, D = (8, 256, 256)
        H = 4 * D
        CAPACITY = 0.5
        b, s, d = x.shape
        weights = (jnp.einsum('bsd,do->bso', x, wr) + br)[..., 0]
        k = max(1, int(CAPACITY * s))
        kk = k - 1 if k > 1 else 1
        _, idx = jax.lax.top_k(weights, k)
        sel_idx = idx[:, :kk]
        sel = jnp.take_along_axis(x, sel_idx[:, :, None], axis=1)
        h = jax.nn.gelu(jnp.einsum('bkd,dh->bkh', sel, w1) + b1)
        y = jnp.einsum('bkh,hd->bkd', h, w2) + b2
        w_sel = jnp.take_along_axis(weights, sel_idx, axis=1)
        y = y * w_sel[..., None]
        batch_idx = jnp.arange(b)[:, None]
        processed = jnp.zeros_like(x).at[batch_idx, sel_idx].set(y)
        return processed + x

    def _L1_gnn_ref(h, norm, weight, gate_weight, src, dst, rel_type):
        import jax, jax.numpy as jnp
        import numpy as np
        N_NODES = 3125
        N_EDGES = 50000
        NUM_RELS = 16
        FEAT = 256
        OUT = 256
        n_nodes = h.shape[0]
        all_msg = jnp.einsum('nf,rfo->rno', h, weight)
        msg = all_msg[rel_type, src] * norm
        all_gate = jnp.einsum('nf,rf->rn', h, gate_weight[..., 0])
        gate = jax.nn.sigmoid(all_gate[rel_type, src])[:, None]
        msg = msg * gate
        agg = jax.ops.segment_sum(msg, dst, num_segments=n_nodes)
        return jax.nn.relu(agg)

    def _L1_ffn_ref(x, Wg, bg, W1, b1, W2, b2):
        import jax, jax.numpy as jnp
        import numpy as np
        TOP_K = 2
        B, L, D = x.shape
        E = W1.shape[0]
        xf = x.reshape(-1, D)
        gate_logits = xf @ Wg + bg
        top_w, top_i = jax.lax.top_k(gate_logits, TOP_K)
        top_w = jax.nn.softmax(top_w, axis=-1)
        w_dense = jnp.sum(jax.nn.one_hot(top_i, E, dtype=xf.dtype) * top_w[..., None], axis=1)
        out = jnp.zeros_like(xf)
        for e in range(E):
            h = jax.nn.gelu(xf @ W1[e] + b1[e], approximate=False)
            out = out + w_dense[:, e:e + 1] * (h @ W2[e] + b2[e])
        return out.reshape(B, L, D)
    x = x + _L0_gnn_ref(_layernorm(x, axis=-1), src, dst, edge_weight, L0_gnn_W, L0_gnn_b)
    x = x + _L0_ffn_ref(_layernorm(x, axis=-1)[None], L0_ffn_attention_mask, L0_ffn_wr, L0_ffn_br, L0_ffn_w1, L0_ffn_b1, L0_ffn_w2, L0_ffn_b2)[0]
    x = x + _L1_gnn_ref(_layernorm(x, axis=-1), edge_weight1, L1_gnn_weight, L1_gnn_gate_weight, src, dst, edge_type_16)
    x = x + _L1_ffn_ref(_layernorm(x, axis=-1)[None], L1_ffn_Wg, L1_ffn_bg, L1_ffn_W1, L1_ffn_b1, L1_ffn_W2, L1_ffn_b2)[0]
    return x

_drawn_inputs = setup_inputs


def setup_inputs(seed=0):
    import zlib

    import numpy as np

    out = dict(_drawn_inputs(seed))
    spreads = {'L0_ffn_b1': (0.0, 0.8),
     'L0_ffn_b2': (0.0, 0.8),
     'L1_ffn_bg': (0.0, 0.361),
     'L1_ffn_b1': (0.0, 0.8),
     'L1_ffn_b2': (0.0, 0.307)}
    factors = {'L0_ffn_wr': 4.804, 'L0_ffn_w1': 5.81, 'L0_ffn_w2': 5.407, 'L1_ffn_W1': 3.671}
    for name, (base, spread) in spreads.items():
        noise = np.random.default_rng([zlib.crc32(name.encode()), seed]).standard_normal(out[name].shape)
        drawn = base * np.exp(spread * noise) if base else spread * noise
        out[name] = jnp.asarray(drawn.astype(out[name].dtype))
    for name, factor in factors.items():
        out[name] = (out[name] * factor).astype(out[name].dtype)
    return out
```

```python
from contextlib import ExitStack

import numpy as np

import concourse.bass as bass
from concourse import mybir

F32 = mybir.dt.float32
F16 = mybir.dt.float16
I32 = mybir.dt.int32
ALU = mybir.AluOpType
ACT = mybir.ActivationFunctionType
AX = mybir.AxisListType

P = 128
D = 256
KC = D // P
NODES = 6250
WINDOWS = -(-NODES // P)
TILES = WINDOWS + WINDOWS % 2
ROWS = TILES * P
EDGES = 100000
EDGE_TILES = -(-EDGES // P)
EDGE_ROWS = EDGE_TILES + 2
RELS = 16
H = 1024
HC = H // P
EXPERTS = 8
TOP = 2
CHOSEN = NODES // 2 - 1
EPS = 1e-5

BATCH = 8
RING = 2 * BATCH
STEPS = -(-(EDGE_TILES + WINDOWS - 1) // RING) * RING
STEP_CHUNKS = -(-(STEPS + 4) // P)
STEP_COLS = STEP_CHUNKS * P
SHIFT = 4

PLACE_TILES = (NODES * TOP + EXPERTS * (P - 1)) // P
PLACE_TILES += PLACE_TILES % 2
PLACES = PLACE_TILES * P

X_SCALE = 2.0 ** 8
W_SCALE = 2.0 ** 10
H_SCALE = 2.0 ** 4
MSG_SCALE = 2.0 ** 6
EDGE_SCALE = 2.0 ** 12
FAR = -3.0e38
STAGES = 4


class Chain:

    def __init__(self, eng, sem, start=0):
        self.eng, self.sem, self.n = eng, sem, start

    def __call__(self, ins):
        self.n += 1
        ins.then_inc(self.sem, 1)
        self.eng.wait_ge(self.sem, self.n)


class Core:

    def __init__(self, nc, ctx):
        self.nc, self.ctx = nc, ctx
        self.at = -(-nc.sbuf_base // 64) * 64
        self.arrived = [self.sem(f"arrived{k}") for k in range(RING)]
        self.held = {e: self.sem(f"{e}_held") for e in ("act", "pool", "dve")}
        self.bank = [ctx.enter_context(nc.psum_tensor(f"bank{i}", [P, 512], F32)) for i in range(8)]

    def sem(self, name):
        return self.ctx.enter_context(self.nc.semaphore(name))

    def sems(self, *names):
        return [self.sem(n) for n in names]

    def sb(self, name, shape, dt, at=None):
        size = int(np.prod(shape[1:])) * mybir.dt.size(dt)
        if at is None:
            at, self.at = self.at, self.at + -(-size // 64) * 64
        assert at + size <= self.nc.sbuf_usable_end, (name, at + size, self.nc.sbuf_usable_end)
        return self.nc.alloc_sbuf_tensor_at(name, shape, dt, offset=at, align_bytes=4)

    def work(self):
        return Work(self)

    def hold(self, eng, which, sem, value):
        eng.wait_ge(sem, value)
        eng.sem_inc(self.held[which], 1)


class Work:
    def __init__(self, core, at=None):
        self.core, self.at = core, core.at if at is None else at

    def sb(self, name, shape, dt):
        size = int(np.prod(shape[1:])) * mybir.dt.size(dt)
        t = self.core.sb(name, shape, dt, at=self.at)
        self.at += -(-size // 64) * 64
        return t


def split_weights(core, loads, scale, name):
    nc = core.nc
    stages = min(STAGES, len(loads))
    loaded = [core.sem(f"{name}_loaded{k}") for k in range(stages)]
    hi_done, lo_done = core.sems(f"{name}_hi_done", f"{name}_lo_done")
    with nc.Block() as block:

        @block.sync
        def _(sp):
            for k, (view, stage, hi, lo, before) in enumerate(loads):
                if before is not None:
                    sp.wait_ge(lo_done, before + 1)
                sp.dma_start(stage, view).then_inc(loaded[k % stages], 16)

        @block.scalar
        def _(act):
            for k, (view, stage, hi, lo, before) in enumerate(loads):
                act.wait_ge(loaded[k % stages], 16 * (k // stages + 1))
                nc.scalar.activation(hi, stage, ACT.Copy, scale=scale).then_inc(hi_done, 1)

        @block.vector
        def _(dve):
            for k, (view, stage, hi, lo, before) in enumerate(loads):
                dve.wait_ge(hi_done, k + 1)
                nc.vector.scalar_tensor_tensor(out=lo, in0=stage, scalar=scale, in1=hi,
                                               op0=ALU.mult, op1=ALU.subtract).then_inc(lo_done, 1)


def tile_of(t, n, width=D):
    return t[:, n * width:(n + 1) * width] if isinstance(n, int) else t[:, bass.ds(n * width, width)]


def col(t, n):
    return t[:, n:n + 1] if isinstance(n, int) else t[:, bass.ds(n, 1)]


def moments(core, name, src, stats, mean, rstd, first=None):
    nc = core.nc
    made, link, root, rooted = core.sems(f"{name}_made", f"{name}_link", f"{name}_root", f"{name}_rooted")
    half, var, tmp = core.ln_tmp
    s6 = stats[:, :].rearrange("p (n s) -> p n s", s=6)
    with nc.Block() as block:

        @block.vector
        def _(dve):
            with dve.Fori(0, TILES) as n:
                if first is not None:
                    first(dve, n).then_inc(made, 1)
                    core.hold(dve, "dve", made, n + 1)
                nc.vector.bn_stats(tile_of(stats, n, 6), tile_of(src, n)).then_inc(link, 1)
            dve.wait_ge(link, TILES)
            chain = Chain(dve, link, TILES)
            chain(nc.vector.tensor_tensor(mean[:, :], s6[:, :, 1], s6[:, :, 4], ALU.add))
            chain(nc.vector.tensor_tensor(half[:, :], s6[:, :, 1], s6[:, :, 4], ALU.subtract))
            chain(nc.vector.tensor_tensor(var[:, :], s6[:, :, 2], s6[:, :, 5], ALU.add))
            chain(nc.vector.tensor_scalar(mean[:, :], mean[:, :], 0.5, None, ALU.mult))
            chain(nc.vector.tensor_tensor(half[:, :], half[:, :], half[:, :], ALU.mult))
            chain(nc.vector.tensor_scalar(var[:, :], var[:, :], 1.0 / D, EPS, ALU.mult, ALU.add))
            chain(nc.vector.scalar_tensor_tensor(out=var[:, :], in0=half[:, :], scalar=0.25, in1=var[:, :],
                                                 op0=ALU.mult, op1=ALU.add))
            dve.sem_inc(root, 1)
            dve.wait_ge(rooted, 1)
            chain(nc.vector.reciprocal(rstd[:, :], tmp[:, :]))
            chain(nc.vector.tensor_tensor(tmp[:, :], rstd[:, :], rstd[:, :], ALU.mult))
            chain(nc.vector.tensor_tensor(tmp[:, :], tmp[:, :], var[:, :], ALU.mult))
            chain(nc.vector.tensor_scalar(tmp[:, :], tmp[:, :], -0.5, 1.5, ALU.mult, ALU.add))
            chain(nc.vector.tensor_tensor(rstd[:, :], rstd[:, :], tmp[:, :], ALU.mult))

        @block.scalar
        def _(act):
            act.wait_ge(root, 1)
            nc.scalar.activation(tmp[:, :], var[:, :], ACT.Sqrt).then_inc(rooted, 1)


def normed(nc, out, src, n, mean, rstd):
    return nc.vector.tensor_scalar(out, tile_of(src, n), col(mean, n), col(rstd, n), ALU.subtract, ALU.mult)


def prepare(core, t, dram):
    nc = core.nc
    w = Work(core)
    last = w.sb("last_dst", [WINDOWS - 1, EDGE_ROWS], I32)
    before = w.sb("before_window", [WINDOWS - 1, EDGE_ROWS], F32)
    ends = w.sb("window_ends", [WINDOWS - 1, 1], F32)
    step_no = w.sb("step_no", [P, STEP_COLS], F32)
    passed = w.sb("windows_passed", [WINDOWS - 1, STEP_COLS], F32)
    win_col = w.sb("win_col", [P, STEP_CHUNKS], F32)
    tile_col = w.sb("tile_col", [P, STEP_CHUNKS], F32)
    tile_idx = w.sb("tile_idx", [P, STEP_CHUNKS], I32)
    low_col = w.sb("low_col", [P, STEP_CHUNKS], F32)
    edges = w.sb("step_edges", [P, STEP_CHUNKS * 5 * P], I32)
    cols = w.sb("step_cols", [P, STEP_CHUNKS * 5 * P], F32)
    half = [w.sb(f"weight_half{g}", [P, STEP_COLS], F16) for g in range(2)]
    loaded, x_loaded, zeroed, iotad, link, steps_known, gathered, ready, turned, emptied, made0 = core.sems(
        "consts_loaded", "x_loaded", "places_zeroed", "iota_made", "prep_link", "steps_known", "edges_gathered",
        "cols_ready", "cols_turned", "cols_emptied", "zeros_made")
    win_ready = core.sem("win_ready")
    per = 10
    with nc.Block() as block:

        @block.sync
        def _(sp):
            sp.dma_start(last[:, :], dram["dst_last"].partition_broadcast(WINDOWS - 1)).then_inc(loaded, 16)
            sp.dma_start(t["ident"][:, :], dram["ident"]).then_inc(loaded, 16)
            sp.dma_start(t["before"][:, :], dram["before"]).then_inc(loaded, 16)
            sp.dma_start(t["valid"][:, :], dram["valid"]).then_inc(loaded, 16)
            sp.dma_start(t["trash"][:, :], dram["trash"]).then_inc(loaded, 16)
            for name in ("b0", "wr", "b2_0"):
                sp.dma_start(t[name][:, :], dram[name].partition_broadcast(P)).then_inc(loaded, 16)
            sp.dma_start(t["br"][:, :], dram["br"].partition_broadcast(P)).then_inc(loaded, 16)
            sp.dma_start(t["bg"][:, :], dram["bg"].partition_broadcast(P)).then_inc(loaded, 16)
            sp.dma_start(t["b1_0"][:, :], dram["b1_0"]).then_inc(loaded, 16)
            acc = t["acc"][:, :].rearrange("p (n d) -> p n d", d=D)
            for k in range(TILES // per):
                rows = dram["x"][k * per * P:(k + 1) * per * P, :]
                sp.dma_start(acc[:, k * per:(k + 1) * per, :], rows.rearrange("(n p) d -> p n d", p=P)).then_inc(x_loaded, 16)
            sp.wait_ge(made0, 1)
            places = dram["places"][0:PLACES, :].rearrange("(n p) d -> p n d", p=P)
            for k in range(0, PLACE_TILES, 2):
                sp.dma_start(places[:, k:k + 2, :], t["zeros"][:, :].rearrange("p (n d) -> p n d", n=2)).then_inc(zeroed, 16)
            sp.wait_ge(x_loaded, 16 * (TILES // per))
            sp.wait_ge(zeroed, 16 * (PLACE_TILES // 2))

        @block.gpsimd
        def _(pool):
            pool.iota(step_no[:, :], pattern=[[1, STEP_COLS]], base=0, channel_multiplier=0,
                      allow_small_or_imprecise_dtypes=True).then_inc(iotad, 1)
            pool.iota(t["part"][:, :], pattern=[[P, STEP_CHUNKS]], base=0, channel_multiplier=1,
                      allow_small_or_imprecise_dtypes=True).then_inc(iotad, 1)
            pool.memset(t["zeros"][:, :], 0.0).then_inc(made0, 1)
            pool.wait_ge(steps_known, 1)
            for k in range(STEP_CHUNKS):
                pool.indirect_dma_start(
                    out=edges[:, k * 5 * P:(k + 1) * 5 * P], out_offset=None, in_=dram["edges"],
                    in_offset=bass.IndirectOffsetOnAxis(ap=tile_idx[:, k:k + 1], axis=0)).then_inc(gathered, 16)

        @block.vector
        def _(dve):
            chain = Chain(dve, link)
            chain(nc.vector.memset(t["ones"][:, :], 1.0))
            dve.wait_ge(iotad, 2)
            dve.wait_ge(loaded, 16 * 11)
            chain(nc.vector.tensor_copy(t["ident16"][:, :], t["ident"][:, :]))
            chain(nc.vector.tensor_copy(t["iota16"][:, :], step_no[:, 0:P]))
            chain(nc.vector.tensor_scalar(ends[:, :], t["part"][0:WINDOWS - 1, 0:1], 128.0, 128.0, ALU.mult, ALU.add))
            chain(nc.vector.tensor_scalar(before[:, :], last[:, :], ends[:, :], None, ALU.is_lt))
            chain(nc.vector.tensor_reduce(ends[:, :], before[:, :], AX.X, ALU.add))
            chain(nc.vector.tensor_tensor(ends[:, :], ends[:, :], t["part"][0:WINDOWS - 1, 0:1], ALU.add))
            chain(nc.vector.tensor_scalar(passed[:, :], step_no[0:WINDOWS - 1, :], ends[:, :], None, ALU.is_gt))
            dve.sem_inc(ready, 1)
            dve.wait_ge(turned, 1)
            chain(nc.vector.tensor_copy(win_col[:, :], core.bank[0][:, 0:STEP_CHUNKS]))
            for k in range(2):
                chain(nc.vector.tensor_copy(t["win"][0:1, k * (STEP_COLS // 2):(k + 1) * (STEP_COLS // 2)],
                                            core.bank[1 + k][0:1, 0:STEP_COLS // 2]))
            chain(nc.vector.tensor_tensor(tile_col[:, :], t["part"][:, :], win_col[:, :], ALU.subtract))
            chain(nc.vector.tensor_scalar(tile_col[:, :], tile_col[:, :], float(EDGE_ROWS - 1), None, ALU.min))
            chain(nc.vector.tensor_scalar(low_col[:, :], win_col[:, :], float(P), None, ALU.mult))
            chain(nc.vector.tensor_copy(tile_idx[:, :], tile_col[:, :]))
            dve.sem_inc(steps_known, 1)
            dve.wait_ge(gathered, 16 * STEP_CHUNKS)
            e = edges[:, :].rearrange("p (k f e) -> p k f e", f=5, e=P)
            c = cols[:, :].rearrange("p (k f e) -> p k f e", f=5, e=P)
            for k in range(STEP_CHUNKS):
                chain(nc.vector.tensor_copy(c[:, k, 0, :], e[:, k, 0, :]))
                chain(nc.vector.scalar_tensor_tensor(out=c[:, k, 1, :], in0=e[:, k, 0, :], scalar=float(RELS),
                                                     in1=e[:, k, 2, :], op0=ALU.mult, op1=ALU.add))
                chain(nc.vector.tensor_scalar(c[:, k, 2, :], e[:, k, 1, :], low_col[:, k:k + 1], None, ALU.subtract))
                chain(nc.vector.tensor_scalar(c[:, k, 3:5, :], e[:, k, 3:5, :].bitcast(F32), EDGE_SCALE, None, ALU.mult))
            dve.sem_inc(ready, 1)
            for k in range(STEP_CHUNKS):
                dve.wait_ge(turned, 2 + k)
                a, b = core.bank[2 * (k % 2)], core.bank[2 * (k % 2) + 1]
                cut = slice(k * P, (k + 1) * P)
                nc.vector.tensor_copy(t["idx0"][:, cut], a[:, 0:P])
                nc.vector.tensor_copy(t["idx1"][:, cut], a[:, P:2 * P])
                nc.vector.tensor_copy(t["local"][:, cut], a[:, 2 * P:3 * P])
                for g, from_ in ((0, a[:, 3 * P:4 * P]), (1, b[:, 0:P])):
                    chain(nc.vector.tensor_copy(half[g][:, cut], from_))
                    chain(nc.vector.tensor_copy(t[f"whi{g}"][:, cut], half[g][:, cut]))
                    nc.vector.tensor_tensor(t[f"wlo{g}"][:, cut], from_, half[g][:, cut], ALU.subtract).then_inc(emptied, 1)

        @block.tensor
        def _(pe):
            pe.wait_ge(ready, 1)
            for k in range(STEP_CHUNKS):
                pe.matmul(core.bank[0][:, k:k + 1], passed[:, k * P:(k + 1) * P], t["ones"][0:WINDOWS - 1, 0:1],
                          start=True, stop=True)
            for k in range(2):
                last_mm = pe.matmul(core.bank[1 + k][0:1, 0:STEP_COLS // 2], t["ones"][0:WINDOWS - 1, 0:1],
                                    passed[:, k * (STEP_COLS // 2):(k + 1) * (STEP_COLS // 2)], start=True, stop=True)
            last_mm.then_inc(turned, 1)
            pe.wait_ge(ready, 2)
            c = cols[:, :].rearrange("p (k f e) -> p k f e", f=5, e=P)
            for k in range(STEP_CHUNKS):
                if k >= 2:
                    pe.wait_ge(emptied, 2 * (k - 1))
                for f in range(5):
                    last_mm = pe.transpose(core.bank[2 * (k % 2) + f // 4][:, (f % 4) * P:(f % 4 + 1) * P],
                                           c[:, k, f, :], t["ident"][:, :])
                last_mm.then_inc(turned, 1)


def table0(core, t, dram, weights):
    nc = core.nc
    w = Work(core, weights)
    xn = [w.sb(f"t0_xn{b}", [P, D], F32) for b in range(2)]
    xT = [w.sb(f"t0_xT{b}", [P, D], F32) for b in range(2)]
    row = [w.sb(f"t0_row{b}", [P, 2 * D], F16) for b in range(2)]
    w0 = w.sb("t0_w0", [P, KC * D], F32)
    loaded, norm_done, turn_done, xT_done, mm_done, hi_done, lo_done, bias_done = core.sems(
        "t0_loaded", "t0_norm_done", "t0_turn_done", "t0_xT_done", "t0_mm_done", "t0_hi_done", "t0_lo_done", "t0_bias_done")
    stored = core.sems("t0_stored0", "t0_stored1")
    psT, psY = core.bank[0:2], core.bank[2:4]
    DEPTH = 2
    tab = dram["table0"].rearrange("(n p) d -> n p d", p=P)
    with nc.Block() as block:

        @block.sync
        def _(sp):
            sp.dma_start(w0[:, :].rearrange("p (c o) -> p c o", c=KC), dram["w0T"].rearrange("(c p) o -> p c o", p=P)).then_inc(loaded, 16)
            with sp.Fori(0, TILES // 2) as i:
                for b in range(2):
                    n = 2 * i + b
                    sp.wait_ge(lo_done, n + 1 + DEPTH)
                    sp.dma_start(dram["table0"][bass.ds(n * P, P), :], row[b][:, :]).then_inc(stored[b], 16)
            for b in range(2):
                sp.wait_ge(stored[b], 16 * (TILES // 2))

        @block.vector
        def _(dve):
            dve.sem_inc(norm_done, DEPTH)
            dve.sem_inc(lo_done, DEPTH)

            def norm(n, b):
                dve.wait_ge(turn_done, n + 1)
                normed(nc, xn[b][:, :], t["acc"], n, t["mean"], t["rstd"]).then_inc(norm_done, 1)

            def low(n, b):
                dve.wait_ge(hi_done, n + 1 + DEPTH)
                nc.vector.scalar_tensor_tensor(out=row[b][:, D:2 * D], in0=psY[b][:, 0:D], scalar=MSG_SCALE,
                                               in1=row[b][:, 0:D], op0=ALU.mult, op1=ALU.subtract).then_inc(lo_done, 1)

            for b in range(2):
                norm(b, b)
            with dve.Fori(0, TILES // 2 - 1) as i:
                for b in range(2):
                    norm(2 * i + 2 + b, b)
                    low(2 * i + b, b)
            for b in range(2):
                low(TILES - 2 + b, b)

        @block.gpsimd
        def _(pool):
            with pool.Fori(0, TILES) as n:
                core.hold(pool, "pool", norm_done, n + 1 + DEPTH)
                nc.gpsimd.tensor_tensor(tile_of(t["acc"], n), tile_of(t["acc"], n), t["b0"][:, :], ALU.add).then_inc(bias_done, 1)
            pool.wait_ge(bias_done, TILES)

        @block.tensor
        def _(pe):
            pe.sem_inc(turn_done, DEPTH)
            pe.sem_inc(mm_done, DEPTH)
            pe.wait_ge(loaded, 16)

            def turn(n, b):
                pe.wait_ge(norm_done, n + 1 + DEPTH)
                pe.wait_ge(xT_done, n + 1)
                for c in range(KC):
                    last = pe.transpose(psT[b][:, c * P:(c + 1) * P], xn[b][:, c * P:(c + 1) * P], t["ident"][:, :])
                last.then_inc(turn_done, 1)

            def product(n, b):
                pe.wait_ge(xT_done, n + 1 + DEPTH)
                pe.wait_ge(lo_done, n + 1)
                for c in range(KC):
                    last = pe.matmul(psY[b][:, 0:D], xT[b][:, c * P:(c + 1) * P], w0[:, c * D:(c + 1) * D],
                                     start=c == 0, stop=c == KC - 1)
                last.then_inc(mm_done, 1)

            for b in range(2):
                turn(b, b)
            with pe.Fori(0, TILES // 2 - 1) as i:
                for b in range(2):
                    product(2 * i + b, b)
                    turn(2 * i + 2 + b, b)
            for b in range(2):
                product(TILES - 2 + b, b)

        @block.scalar
        def _(act):
            act.sem_inc(xT_done, DEPTH)
            act.sem_inc(hi_done, DEPTH)

            def copy(n, b):
                act.wait_ge(turn_done, n + 1 + DEPTH)
                act.wait_ge(mm_done, n + 1)
                nc.scalar.activation(xT[b][:, :], psT[b][:, 0:D], ACT.Copy).then_inc(xT_done, 1)

            def high(n, b):
                act.wait_ge(mm_done, n + 1 + DEPTH)
                core.hold(act, "act", stored[b], (n - b) * 8)
                nc.scalar.activation(row[b][:, 0:D], psY[b][:, 0:D], ACT.Copy, scale=MSG_SCALE).then_inc(hi_done, 1)

            for b in range(2):
                copy(b, b)
            with act.Fori(0, TILES // 2 - 1) as i:
                for b in range(2):
                    high(2 * i + b, b)
                    copy(2 * i + 2 + b, b)
            for b in range(2):
                high(TILES - 2 + b, b)


def gather(core, t, table, g, acc, weights):
    nc = core.nc
    w = Work(core, weights)
    name = f"g{g}"
    rounds = STEPS // RING
    msg = [w.sb(f"{name}_msg{k}", [P, 2 * D], F16) for k in range(RING)]
    idx = [w.sb(f"{name}_idx{b}", [P, BATCH], I32) for b in range(2)]
    hot = [w.sb(f"{name}_hot{k}", [P, 2 * P], F16) for k in range(4)]
    arrived, before = core.arrived, g * rounds
    idx_done, hot_done, mm_done, sum_done = core.sems(f"{name}_idx_done", f"{name}_hot_done", f"{name}_mm_done", f"{name}_sum_done")
    HOT, PS, AHEAD = 4, 4, 2
    ps = core.bank[0:PS]
    whi, wlo, local, win = t[f"whi{g}"], t[f"wlo{g}"], t["local"], t["win"]
    with nc.Block() as block:

        @block.gpsimd
        def _(pool):
            with pool.Fori(0, rounds) as i:
                for b in range(2):
                    m = 2 * i + b
                    core.hold(pool, "pool", mm_done, m * BATCH + BATCH)
                    pool.tensor_copy(idx[b][:, :], t[f"idx{g}"][:, bass.ds(m * BATCH, BATCH)]).then_inc(idx_done, 1)
                    core.hold(pool, "pool", idx_done, m + 1)
                    for k in range(BATCH):
                        pool.indirect_dma_start(
                            out=msg[b * BATCH + k][:, :], out_offset=None, in_=table,
                            in_offset=bass.IndirectOffsetOnAxis(ap=idx[b][:, k:k + 1], axis=0)).then_inc(arrived[b * BATCH + k], 16)

        @block.vector
        def _(dve):
            dve.sem_inc(sum_done, PS)
            dve.sem_inc(hot_done, HOT)

            def one_hot(s, k):
                dve.wait_ge(mm_done, s + RING - HOT + 1)
                nc.vector.tensor_scalar(hot[k % HOT][:, 0:P], t["iota16"][:, :], col(local, s), col(whi, s), ALU.is_equal, ALU.mult)
                nc.vector.tensor_scalar(hot[k % HOT][:, P:2 * P], t["iota16"][:, :], col(local, s), col(wlo, s), ALU.is_equal,
                                        ALU.mult).then_inc(hot_done, 1)

            def add(s, k):
                at = dve.value_load(win[0:1, bass.ds(s, 1)], min_val=0, max_val=WINDOWS - 1)
                part = acc[:, bass.ds(at * D, D)]
                dve.wait_ge(mm_done, s + RING + 1)
                dve.wait_ge(sum_done, s + PS)
                nc.vector.scalar_tensor_tensor(out=part, in0=ps[k % PS][:, 0:D], scalar=1.0 / (MSG_SCALE * EDGE_SCALE), in1=part,
                                               op0=ALU.mult, op1=ALU.add).then_inc(sum_done, 1)

            for k in range(AHEAD):
                one_hot(k, k)
            with dve.Fori(0, rounds) as i:
                for k in range(RING):
                    one_hot(i * RING + k + AHEAD, k + AHEAD)
                    add(i * RING + k, k)

        @block.tensor
        def _(pe):
            pe.sem_inc(mm_done, RING)
            with pe.Fori(0, rounds) as i:
                for k in range(RING):
                    s = i * RING + k
                    pe.wait_ge(hot_done, s + 1 + HOT)
                    pe.wait_ge(sum_done, s + 1)
                    pe.wait_ge(arrived[k], 16 * (before + i + 1))
                    hi, lo = hot[k % HOT][:, 0:P], hot[k % HOT][:, P:2 * P]
                    pe.matmul(ps[k % PS][:, 0:D], hi, msg[k][:, 0:D], start=True, stop=False)
                    pe.matmul(ps[k % PS][:, 0:D], hi, msg[k][:, D:2 * D], start=False, stop=False)
                    pe.matmul(ps[k % PS][:, 0:D], lo, msg[k][:, 0:D], start=False, stop=True).then_inc(mm_done, 1)


def ffn0(core, t, free, w1, w2):
    nc = core.nc
    w = Work(core, free)
    pair = lambda name, cols, dt: [w.sb(f"f0_{name}{b}", [P, cols], dt) for b in range(2)]
    xn, junk, dot = pair("xn", D, F32), pair("junk", D, F32), pair("dot", 1, F32)
    xhi, xlo = pair("xhi", D, F16), pair("xlo", D, F16)
    g, ghi, glo = pair("g", H, F32), pair("ghi", H, F16), pair("glo", H, F16)
    norm_done, dot_done, routed, added, turned, xhi_done, xlo_done, up_done, gelu_done, ghi_done, glo_done, down_done, out_done = core.sems(
        "f0_norm_done", "f0_dot_done", "f0_routed", "f0_added", "f0_turned", "f0_xhi_done", "f0_xlo_done", "f0_up_done", "f0_gelu_done",
        "f0_ghi_done", "f0_glo_done", "f0_down_done", "f0_out_done")
    psT, psY = core.bank[0:2], core.bank[6:8]
    psH = [core.bank[2:4], core.bank[4:6]]
    DEPTH = 2
    LEAD = 3

    def slots(eng, slot):
        body = TILES - LEAD - (TILES - LEAD) % 2
        with eng.Fori(0, body // 2) as i:
            for b in range(2):
                slot(2 * i + b, b, TILES)
        for n in range(body, TILES):
            slot(n, n % 2, TILES - n)

    with nc.Block() as block:

        @block.vector
        def _(dve):
            for s in (norm_done, dot_done, routed, xlo_done, glo_done, out_done):
                dve.sem_inc(s, DEPTH)

            def norm(n, b):
                dve.wait_ge(turned, n + 1)
                dve.wait_ge(added, n + 1)
                dve.wait_ge(dot_done, n + 1)
                normed(nc, xn[b][:, :], t["acc"], n, t["mean"], t["rstd"]).then_inc(norm_done, 1)

            def route(n, b):
                dve.wait_ge(norm_done, n + 1 + DEPTH)
                dve.wait_ge(routed, n + 1)
                nc.vector.tensor_tensor_reduce(out=junk[b][:, :], in0=xn[b][:, :], in1=t["wr"][:, :], scale=1.0, scalar=0.0,
                                               op0=ALU.mult, op1=ALU.add, accum_out=dot[b][:, :]).then_inc(dot_done, 1)
                dve.wait_ge(dot_done, n + 1 + DEPTH)
                nc.vector.tensor_scalar(col(t["router"], n), dot[b][:, :], t["br"][:, :], None, ALU.add).then_inc(routed, 1)

            def xlow(n, b):
                dve.wait_ge(xhi_done, n + 1 + DEPTH)
                nc.vector.scalar_tensor_tensor(out=xlo[b][:, :], in0=psT[b][:, 0:D], scalar=X_SCALE, in1=xhi[b][:, :],
                                               op0=ALU.mult, op1=ALU.subtract).then_inc(xlo_done, 1)

            def glow(n, b):
                dve.wait_ge(ghi_done, n + 1 + DEPTH)
                nc.vector.scalar_tensor_tensor(out=glo[b][:, :], in0=g[b][:, :], scalar=H_SCALE, in1=ghi[b][:, :],
                                               op0=ALU.mult, op1=ALU.subtract).then_inc(glo_done, 1)

            def result(n, b):
                dve.wait_ge(down_done, n + 1 + DEPTH)
                nc.vector.scalar_tensor_tensor(out=tile_of(t["side"], n), in0=psY[b][:, 0:D], scalar=1.0 / (H_SCALE * W_SCALE),
                                               in1=t["b2_0"][:, :], op0=ALU.mult, op1=ALU.add).then_inc(out_done, 1)

            def slot(n, b, left):
                if left > 3:
                    norm(n + 3, 1 - b)
                glow(n, b)
                if left > 2:
                    xlow(n + 2, b)
                if left > 3:
                    route(n + 3, 1 - b)
                result(n, b)

            for n in range(2):
                norm(n, n)
                route(n, n)
            for n in range(2):
                xlow(n, n)
            norm(2, 0)
            route(2, 0)
            slots(dve, slot)

        @block.gpsimd
        def _(pool):
            pool.sem_inc(added, DEPTH)
            pool.sem_inc(ghi_done, DEPTH)

            def add(n, b):
                core.hold(pool, "pool", norm_done, n + 1 + DEPTH)
                nc.gpsimd.tensor_tensor(tile_of(t["acc"], n), tile_of(t["acc"], n), xn[b][:, :], ALU.add).then_inc(added, 1)

            def ghigh(n, b):
                core.hold(pool, "pool", glo_done, n + 1)
                core.hold(pool, "pool", down_done, n + 1)
                core.hold(pool, "pool", gelu_done, n + 1 + DEPTH)
                nc.gpsimd.tensor_scalar(ghi[b][:, :], g[b][:, :], H_SCALE, None, ALU.mult).then_inc(ghi_done, 1)

            def slot(n, b, left):
                ghigh(n, b)
                if left > 2:
                    add(n + 2, b)

            for n in range(2):
                add(n, n)
            slots(pool, slot)

        @block.scalar
        def _(act):
            act.sem_inc(xhi_done, DEPTH)
            act.sem_inc(gelu_done, DEPTH)

            def xhigh(n, b):
                core.hold(act, "act", up_done, n + 1)
                core.hold(act, "act", turned, n + 1 + DEPTH)
                nc.scalar.activation(xhi[b][:, :], psT[b][:, 0:D], ACT.Copy, scale=X_SCALE).then_inc(xhi_done, 1)

            def gelu(n, b):
                core.hold(act, "act", glo_done, n + 1)
                core.hold(act, "act", up_done, n + 1 + DEPTH)
                for c in range(HC):
                    last = nc.scalar.activation(g[b][:, c * P:(c + 1) * P], psH[b][c // 4][:, (c % 4) * P:(c % 4 + 1) * P],
                                                ACT.Gelu_apprx_tanh, bias=t["b1_0"][:, c:c + 1], scale=1.0 / (X_SCALE * W_SCALE))
                last.then_inc(gelu_done, 1)

            def slot(n, b, left):
                if left > 2:
                    xhigh(n + 2, b)
                if left > 1:
                    gelu(n + 1, 1 - b)

            for n in range(2):
                xhigh(n, n)
            gelu(0, 0)
            slots(act, slot)

        @block.tensor
        def _(pe):
            for s in (turned, up_done, down_done):
                pe.sem_inc(s, DEPTH)

            def turn(n, b):
                pe.wait_ge(xlo_done, n + 1)
                pe.wait_ge(norm_done, n + 1 + DEPTH)
                for c in range(KC):
                    last = pe.transpose(psT[b][:, c * P:(c + 1) * P], xn[b][:, c * P:(c + 1) * P], t["ident"][:, :])
                last.then_inc(turned, 1)

            def up(n, b):
                pe.wait_ge(gelu_done, n + 1)
                pe.wait_ge(xlo_done, n + 1 + DEPTH)
                for c in range(HC):
                    out = psH[b][c // 4][:, (c % 4) * P:(c % 4 + 1) * P]
                    for k in range(KC):
                        whi, wlo = (w1[j][:, k * H + c * P:k * H + (c + 1) * P] for j in range(2))
                        hi, lo = xhi[b][:, k * P:(k + 1) * P], xlo[b][:, k * P:(k + 1) * P]
                        pe.matmul(out, whi, hi, start=k == 0, stop=False)
                        pe.matmul(out, whi, lo, start=False, stop=False)
                        last = pe.matmul(out, wlo, hi, start=False, stop=k == KC - 1)
                last.then_inc(up_done, 1)

            def down(n, b):
                pe.wait_ge(out_done, n + 1)
                pe.wait_ge(glo_done, n + 1 + DEPTH)
                for c in range(HC):
                    hi, lo = ghi[b][:, c * P:(c + 1) * P], glo[b][:, c * P:(c + 1) * P]
                    whi, wlo = (w2[j][:, c * D:(c + 1) * D] for j in range(2))
                    pe.matmul(psY[b][:, 0:D], hi, whi, start=c == 0, stop=False)
                    pe.matmul(psY[b][:, 0:D], hi, wlo, start=False, stop=False)
                    last = pe.matmul(psY[b][:, 0:D], lo, whi, start=False, stop=c == HC - 1)
                last.then_inc(down_done, 1)

            def slot(n, b, left):
                if left > 2:
                    turn(n + 2, b)
                if left > 1:
                    up(n + 1, 1 - b)
                down(n, b)

            for n in range(2):
                turn(n, n)
            up(0, 0)
            slots(pe, slot)


def scan_tiles(chain, nc, a, b, width):
    step = 1
    while step < TILES:
        chain(nc.vector.tensor_copy(b[:, 0:step * width], a[:, 0:step * width]))
        chain(nc.vector.tensor_tensor(b[:, step * width:TILES * width], a[:, step * width:TILES * width],
                                      a[:, 0:(TILES - step) * width], ALU.add))
        a, b, step = b, a, 2 * step
    return a


def choose(core, t, free):
    nc = core.nc
    w = Work(core, free)
    u, hits, ties, total, scan, bad = (w.sb(f"ch_{k}", [P, TILES], F32) for k in ("u", "hits", "ties", "total", "scan", "bad"))
    count, rank, sign, bit_f, need = (w.sb(f"ch_{k}", [P, 1], F32) for k in ("count", "rank", "sign", "bit_f", "need"))
    bits, cand, keep, bit = (w.sb(f"ch_{k}", [P, 1], I32) for k in ("bits", "cand", "keep", "bit"))
    link, counted, summed, loop_link, bit_link = core.sems("ch_link", "ch_counted", "ch_summed", "ch_loop_link", "ch_bit_link")
    ROUNDS = 31
    ps = core.bank[0]
    with nc.Block() as block:

        @block.vector
        def _(dve):
            chain = Chain(dve, link)

            def everywhere(n):
                dve.sem_inc(counted, 1)
                dve.wait_ge(summed, n)

            chain(nc.vector.tensor_scalar(bad[:, :], t["valid"][:, :], -1.0, -FAR, ALU.add, ALU.mult))
            chain(nc.vector.tensor_scalar(hits[:, :], t["router"][:, :], 0.0, None, ALU.is_ge))
            chain(nc.vector.tensor_tensor(hits[:, :], hits[:, :], t["valid"][:, :], ALU.mult))
            chain(nc.vector.tensor_reduce(count[:, :], hits[:, :], AX.X, ALU.add))
            everywhere(1)
            chain(nc.vector.tensor_scalar(rank[:, :], ps[:, 0:1], float(CHOSEN), None, ALU.is_lt))
            chain(nc.vector.tensor_scalar(sign[:, :], rank[:, :], -2.0, 1.0, ALU.mult, ALU.add))
            chain(nc.vector.tensor_scalar(rank[:, :], rank[:, :], float(NODES + 1 - 2 * CHOSEN), float(CHOSEN), ALU.mult, ALU.add))
            chain(nc.vector.tensor_scalar(u[:, :], t["router"][:, :], sign[:, :], None, ALU.mult))
            chain(nc.vector.tensor_tensor(u[:, :], u[:, :], t["valid"][:, :], ALU.mult))
            chain(nc.vector.tensor_tensor(u[:, :], u[:, :], bad[:, :], ALU.add))
            chain(nc.vector.memset(bits[:, :], 0))
            chain(nc.vector.memset(bit_f[:, :], 2.0 ** (ROUNDS - 1)))
            chain(nc.vector.tensor_copy(bit[:, :], bit_f[:, :]))
            PER = 5
            with dve.Fori(0, ROUNDS) as r:
                dve.wait_ge(loop_link, r * PER)
                nc.vector.tensor_tensor(cand[:, :], bits[:, :], bit[:, :], ALU.bitwise_or).then_inc(loop_link, 1)
                dve.wait_ge(loop_link, r * PER + 1)
                nc.vector.tensor_scalar(hits[:, :], u[:, :], cand[:, :].bitcast(F32), None, ALU.is_ge).then_inc(loop_link, 1)
                dve.wait_ge(loop_link, r * PER + 2)
                nc.vector.tensor_reduce(count[:, :], hits[:, :], AX.X, ALU.add).then_inc(counted, 1)
                dve.wait_ge(summed, r + 2)
                nc.vector.scalar_tensor_tensor(out=keep[:, :], in0=ps[:, 0:1], scalar=rank[:, :], in1=bit_f[:, :],
                                               op0=ALU.is_ge, op1=ALU.mult).then_inc(loop_link, 1)
                dve.wait_ge(loop_link, r * PER + 3)
                nc.vector.tensor_tensor(bits[:, :], bits[:, :], keep[:, :], ALU.bitwise_or).then_inc(loop_link, 1)
                nc.vector.tensor_scalar(bit_f[:, :], bit_f[:, :], 0.5, None, ALU.mult).then_inc(bit_link, 1)
                dve.wait_ge(bit_link, r + 1)
                nc.vector.tensor_copy(bit[:, :], bit_f[:, :]).then_inc(loop_link, 1)
            dve.wait_ge(loop_link, ROUNDS * PER)
            chain(nc.vector.tensor_scalar(sign[:, :], sign[:, :], bits[:, :].bitcast(F32), None, ALU.mult))
            chain(nc.vector.tensor_scalar(ties[:, :], t["router"][:, :], sign[:, :], None, ALU.is_equal))
            chain(nc.vector.tensor_tensor(ties[:, :], ties[:, :], t["valid"][:, :], ALU.mult))
            chain(nc.vector.tensor_scalar(hits[:, :], t["router"][:, :], sign[:, :], None, ALU.is_gt))
            chain(nc.vector.tensor_tensor(hits[:, :], hits[:, :], t["valid"][:, :], ALU.mult))
            chain(nc.vector.tensor_reduce(count[:, :], hits[:, :], AX.X, ALU.add))
            everywhere(ROUNDS + 2)
            chain(nc.vector.tensor_scalar(need[:, :], ps[:, 0:1], -1.0, float(CHOSEN), ALU.mult, ALU.add))
            chain(nc.vector.tensor_copy(total[:, :], core.bank[1][:, 0:TILES]))
            run = scan_tiles(chain, nc, total, scan, 1)
            chain(nc.vector.tensor_tensor(run[:, :], run[:, :], core.bank[1][:, 0:TILES], ALU.subtract))
            chain(nc.vector.tensor_tensor(run[:, :], run[:, :], core.bank[2][:, 0:TILES], ALU.add))
            chain(nc.vector.tensor_scalar(run[:, :], run[:, :], need[:, :], None, ALU.is_lt))
            chain(nc.vector.tensor_tensor(ties[:, :], ties[:, :], run[:, :], ALU.mult))
            chain(nc.vector.tensor_tensor(hits[:, :], hits[:, :], ties[:, :], ALU.add))
            chain(nc.vector.tensor_tensor(t["chosen"][:, :], hits[:, :], t["router"][:, :], ALU.mult))

        @block.tensor
        def _(pe):
            pe.wait_ge(counted, 1)
            pe.matmul(ps[:, 0:1], t["ones"][:, :], count[:, :], start=True, stop=True).then_inc(summed, 1)
            with pe.Fori(0, ROUNDS) as r:
                pe.wait_ge(counted, r + 2)
                pe.matmul(ps[:, 0:1], t["ones"][:, :], count[:, :], start=True, stop=True).then_inc(summed, 1)
            pe.wait_ge(counted, ROUNDS + 2)
            pe.matmul(core.bank[1][:, 0:TILES], t["ones"][:, :], ties[:, :], start=True, stop=True)
            pe.matmul(core.bank[2][:, 0:TILES], t["before"][:, :], ties[:, :], start=True, stop=True)
            pe.matmul(ps[:, 0:1], t["ones"][:, :], count[:, :], start=True, stop=True).then_inc(summed, 1)


def table1(core, t, dram, free, wrel, wgate):
    nc = core.nc
    w = Work(core, free)
    pair = lambda name, cols, dt: [w.sb(f"t1_{name}{b}", [P, cols], dt) for b in range(2)]
    xn, xhi, xlo = pair("xn", D, F32), pair("xhi", D, F16), pair("xlo", D, F16)
    raw, gate, row = pair("raw", RELS, F32), pair("gate", RELS, F32), pair("row", RELS * 2 * D, F16)
    norm_done, turned, xhi_done, xlo_done, logit_done, raw_done, gate_done, rel_done, hi_done, lo_done, side_zeroed = core.sems(
        "t1_norm_done", "t1_turned", "t1_xhi_done", "t1_xlo_done", "t1_logit_done", "t1_raw_done", "t1_gate_done", "t1_rel_done",
        "t1_hi_done", "t1_lo_done", "side_zeroed")
    stored = core.sems("t1_stored0", "t1_stored1")
    psT, psG, psR = core.bank[0:2], core.bank[2:4], core.bank[4:8]
    DEPTH = 2
    PAIRS = RELS // 2
    tab = dram["table1"].rearrange("(n r) d -> n (r d)", r=RELS)

    def slots(eng, slot):
        with eng.Fori(0, TILES // 2 - 1) as i:
            for b in range(2):
                slot(2 * i + b, b, 2)
        slot(TILES - 2, 0, 1)
        slot(TILES - 1, 1, 0)

    with nc.Block() as block:

        @block.gpsimd
        def _(pool):
            pool.memset(t["side"][:, :], 0.0).then_inc(side_zeroed, 1)
            pool.wait_ge(side_zeroed, 1)

        @block.sync
        def _(sp):
            with sp.Fori(0, TILES // 2) as i:
                for b in range(2):
                    n = 2 * i + b
                    sp.wait_ge(lo_done, (n + 1 + DEPTH) * RELS)
                    sp.dma_start(tab[bass.ds(n * P, P), :], row[b][:, :]).then_inc(stored[b], 16)
            for b in range(2):
                sp.wait_ge(stored[b], 16 * (TILES // 2))

        @block.vector
        def _(dve):
            for s, n in ((norm_done, DEPTH), (xlo_done, DEPTH), (gate_done, DEPTH), (lo_done, DEPTH * RELS)):
                dve.sem_inc(s, n)

            def norm(n, b):
                dve.wait_ge(turned, n + 1)
                normed(nc, xn[b][:, :], t["acc"], n, t["mean"], t["rstd"]).then_inc(norm_done, 1)

            def xlow(n, b):
                dve.wait_ge(xhi_done, n + 1 + DEPTH)
                nc.vector.scalar_tensor_tensor(out=xlo[b][:, :], in0=psT[b][:, 0:D], scalar=X_SCALE, in1=xhi[b][:, :],
                                               op0=ALU.mult, op1=ALU.subtract).then_inc(xlo_done, 1)

            def scale_gate(n, b):
                dve.wait_ge(lo_done, (n - 1 + DEPTH) * RELS)
                dve.wait_ge(raw_done, n + 1 + DEPTH)
                nc.vector.tensor_scalar(gate[b][:, :], raw[b][:, :], MSG_SCALE / (X_SCALE * W_SCALE), None, ALU.mult).then_inc(gate_done, 1)

            def low(n, b, r):
                if r % 2 == 0:
                    dve.wait_ge(hi_done, (n + DEPTH) * RELS + r + 2)
                at = psR[r // 2 % 4][:, (r % 2) * D:(r % 2 + 1) * D]
                hi, lo = (row[b][:, (2 * r + j) * D:(2 * r + j + 1) * D] for j in range(2))
                nc.vector.scalar_tensor_tensor(out=lo, in0=at, scalar=gate[b][:, r:r + 1], in1=hi,
                                               op0=ALU.mult, op1=ALU.subtract).then_inc(lo_done, 1)

            def slot(n, b, more):
                if more > 1:
                    norm(n + 2, b)
                if more:
                    xlow(n + 1, 1 - b)
                for r in range(RELS):
                    low(n, b, r)
                    if r == RELS // 2 + 1 and more:
                        scale_gate(n + 1, 1 - b)

            norm(0, 0)
            norm(1, 1)
            xlow(0, 0)
            scale_gate(0, 0)
            slots(dve, slot)

        @block.scalar
        def _(act):
            for s, n in ((xhi_done, DEPTH), (raw_done, DEPTH), (hi_done, DEPTH * RELS)):
                act.sem_inc(s, n)

            def xhigh(n, b):
                core.hold(act, "act", rel_done, (n - 1 + DEPTH) * PAIRS)
                core.hold(act, "act", turned, n + 1 + DEPTH)
                nc.scalar.activation(xhi[b][:, :], psT[b][:, 0:D], ACT.Copy, scale=X_SCALE).then_inc(xhi_done, 1)

            def sigmoid(n, b):
                core.hold(act, "act", gate_done, n + 1)
                core.hold(act, "act", logit_done, n + 1 + DEPTH)
                nc.scalar.activation(raw[b][:, :], psG[b][:, 0:RELS], ACT.Sigmoid, scale=1.0 / (X_SCALE * W_SCALE)).then_inc(raw_done, 1)

            def high(n, b, r):
                if r == 0:
                    core.hold(act, "act", gate_done, n + 1 + DEPTH)
                    core.hold(act, "act", stored[b], (n - b) * 8)
                if r % 2 == 0:
                    core.hold(act, "act", rel_done, (n + DEPTH) * PAIRS + r // 2 + 1)
                at = psR[r // 2 % 4][:, (r % 2) * D:(r % 2 + 1) * D]
                nc.scalar.activation(row[b][:, 2 * r * D:(2 * r + 1) * D], at, ACT.Copy, scale=gate[b][:, r:r + 1]).then_inc(hi_done, 1)

            def slot(n, b, more):
                if more:
                    xhigh(n + 1, 1 - b)
                for r in range(RELS):
                    high(n, b, r)
                    if r == RELS // 2 - 1 and more:
                        sigmoid(n + 1, 1 - b)

            xhigh(0, 0)
            sigmoid(0, 0)
            slots(act, slot)

        @block.tensor
        def _(pe):
            for s, n in ((turned, DEPTH), (logit_done, DEPTH), (rel_done, DEPTH * PAIRS)):
                pe.sem_inc(s, n)

            def turn(n, b):
                pe.wait_ge(xlo_done, n + 1)
                pe.wait_ge(norm_done, n + 1 + DEPTH)
                for c in range(KC):
                    last = pe.transpose(psT[b][:, c * P:(c + 1) * P], xn[b][:, c * P:(c + 1) * P], t["ident"][:, :])
                last.then_inc(turned, 1)

            def product(out, b, right):
                for k in range(KC):
                    hi, lo = xhi[b][:, k * P:(k + 1) * P], xlo[b][:, k * P:(k + 1) * P]
                    rhi, rlo = right(0, k), right(1, k)
                    nc.tensor.matmul(out, hi, rhi, start=k == 0, stop=False)
                    nc.tensor.matmul(out, hi, rlo, start=False, stop=False)
                    last = nc.tensor.matmul(out, lo, rhi, start=False, stop=k == KC - 1)
                return last

            def logits(n, b):
                pe.wait_ge(raw_done, n + 1)
                pe.wait_ge(xlo_done, n + 1 + DEPTH)
                product(psG[b][:, 0:RELS], b, lambda j, k: wgate[j][:, k * RELS:(k + 1) * RELS]).then_inc(logit_done, 1)

            def relations(n, b, q):
                pe.wait_ge(lo_done, (n + DEPTH) * RELS + 2 * (q + 1 - 4))
                at = lambda j, k: wrel[j][:, (k * RELS + 2 * q) * D:(k * RELS + 2 * q + 2) * D]
                product(psR[q % 4][:, :], b, at).then_inc(rel_done, 1)

            def slot(n, b, more):
                if more:
                    turn(n + 1, 1 - b)
                for q in range(PAIRS):
                    relations(n, b, q)
                    if q == PAIRS // 2 - 1 and more:
                        logits(n + 1, 1 - b)

            turn(0, 0)
            logits(0, 0)
            slots(pe, slot)


def score(core, t, dram, free, logits):
    nc = core.nc
    w = Work(core, free)
    xn = [w.sb(f"sc_xn{b}", [P, D], F32) for b in range(2)]
    xT = [w.sb(f"sc_xT{b}", [P, D], F32) for b in range(2)]
    wg = w.sb("sc_wg", [P, KC * EXPERTS], F32)
    loaded, norm_done, turned, xT_done, mm_done, out_done, x_stored = core.sems(
        "sc_loaded", "sc_norm_done", "sc_turned", "sc_xT_done", "sc_mm_done", "sc_out_done", "x_stored")
    psT, psL = core.bank[0:2], core.bank[2:4]
    DEPTH = 2
    with nc.Block() as block:

        @block.sync
        def _(sp):
            sp.dma_start(wg[:, :].rearrange("p (c e) -> p c e", c=KC), dram["wg"].rearrange("(c p) e -> p c e", p=P)).then_inc(loaded, 16)
            sp.dma_start(dram["x3"].rearrange("(n p) d -> p n d", p=P), t["acc"][:, :].rearrange("p (n d) -> p n d", d=D)).then_inc(x_stored, 16)
            sp.wait_ge(x_stored, 16)

        @block.vector
        def _(dve):
            dve.sem_inc(norm_done, DEPTH)
            dve.sem_inc(out_done, DEPTH)

            def norm(n, b):
                dve.wait_ge(turned, n + 1)
                normed(nc, xn[b][:, :], t["acc"], n, t["mean"], t["rstd"]).then_inc(norm_done, 1)

            def result(n, b):
                dve.wait_ge(mm_done, n + 1 + DEPTH)
                nc.vector.tensor_tensor(tile_of(logits, n, EXPERTS), psL[b][:, 0:EXPERTS], t["bg"][:, :], ALU.add).then_inc(out_done, 1)

            for b in range(2):
                norm(b, b)
            with dve.Fori(0, TILES // 2 - 1) as i:
                for b in range(2):
                    norm(2 * i + 2 + b, b)
                    result(2 * i + b, b)
            for b in range(2):
                result(TILES - 2 + b, b)

        @block.tensor
        def _(pe):
            pe.sem_inc(turned, DEPTH)
            pe.sem_inc(mm_done, DEPTH)
            pe.wait_ge(loaded, 16)

            def turn(n, b):
                pe.wait_ge(norm_done, n + 1 + DEPTH)
                pe.wait_ge(xT_done, n + 1)
                for c in range(KC):
                    last = pe.transpose(psT[b][:, c * P:(c + 1) * P], xn[b][:, c * P:(c + 1) * P], t["ident"][:, :])
                last.then_inc(turned, 1)

            def product(n, b):
                pe.wait_ge(xT_done, n + 1 + DEPTH)
                pe.wait_ge(out_done, n + 1)
                for c in range(KC):
                    last = pe.matmul(psL[b][:, 0:EXPERTS], xT[b][:, c * P:(c + 1) * P], wg[:, c * EXPERTS:(c + 1) * EXPERTS],
                                     start=c == 0, stop=c == KC - 1)
                last.then_inc(mm_done, 1)

            for b in range(2):
                turn(b, b)
            with pe.Fori(0, TILES // 2 - 1) as i:
                for b in range(2):
                    product(2 * i + b, b)
                    turn(2 * i + 2 + b, b)
            for b in range(2):
                product(TILES - 2 + b, b)

        @block.scalar
        def _(act):
            act.sem_inc(xT_done, DEPTH)

            def copy(n, b):
                act.wait_ge(turned, n + 1 + DEPTH)
                act.wait_ge(mm_done, n + 1)
                nc.scalar.activation(xT[b][:, :], psT[b][:, 0:D], ACT.Copy).then_inc(xT_done, 1)

            for b in range(2):
                copy(b, b)
            with act.Fori(0, TILES // 2 - 1) as i:
                for b in range(2):
                    copy(2 * i + 2 + b, b)


def place(core, t, free, logits):
    nc = core.nc
    w = Work(core, free)
    wide = [w.sb(f"pl_wide{k}", [P, TILES * EXPERTS * EXPERTS], F32) for k in range(2)]
    rank, picked, total, scan, masked = (w.sb(f"pl_{k}", [P, TILES * EXPERTS], F32) for k in ("rank", "picked", "total", "scan", "masked"))
    best = [w.sb(f"pl_best{k}", [P, TILES], F32) for k in range(TOP)]
    pos = w.sb("pl_pos", [P, TILES], F32)
    one = w.sb("pl_one", [P, TILES], F32)
    count, full, start = (w.sb(f"pl_{k}", [P, EXPERTS], F32) for k in ("count", "full", "start"))
    full_i = w.sb("pl_full_i", [P, EXPERTS], I32)
    tile_no = w.sb("pl_tile_no", [1, PLACE_TILES], F32)
    over = w.sb("pl_over", [1, PLACE_TILES * EXPERTS], F32)
    owner = w.sb("pl_owner", [1, PLACE_TILES], F32)
    earlier = w.sb("pl_earlier", [P, EXPERTS * EXPERTS], F32)
    link, numbered, picks_ready, exped, exp_ready, summed = core.sems(
        "pl_link", "pl_numbered", "pl_picks_ready", "pl_exped", "pl_exp_ready", "pl_summed")
    psB, psT = core.bank[0], core.bank[1]
    TE = TILES * EXPERTS
    with nc.Block() as block:

        @block.gpsimd
        def _(pool):
            pool.iota(tile_no[:, :], pattern=[[P, PLACE_TILES]], base=0, channel_multiplier=0,
                      allow_small_or_imprecise_dtypes=True).then_inc(numbered, 1)

        @block.vector
        def _(dve):
            chain = Chain(dve, link)
            l3 = logits[:, :].rearrange("p (n e) -> p n e", e=EXPERTS)
            w4 = [x[:, :].rearrange("p (n e j) -> p n e j", e=EXPERTS, j=EXPERTS) for x in wide]
            shape = [P, TILES, EXPERTS, EXPERTS]
            of_j, of_e = l3.unsqueeze(2).to_broadcast(shape), l3.unsqueeze(3).to_broadcast(shape)
            r3 = rank[:, :].rearrange("p (n e) -> p n e", e=EXPERTS)
            e2 = earlier[:, :].rearrange("p (e j) -> p e j", j=EXPERTS)
            chain(nc.vector.memset(earlier[:, :], 0.0))
            for e in range(1, EXPERTS):
                chain(nc.vector.memset(earlier[:, e * EXPERTS:e * EXPERTS + e], 1.0))
            chain(nc.vector.tensor_tensor(w4[0], of_j, of_e, ALU.is_equal))
            chain(nc.vector.tensor_tensor(w4[0], w4[0], e2.unsqueeze(1).to_broadcast(shape), ALU.mult))
            chain(nc.vector.tensor_tensor(w4[1], of_j, of_e, ALU.is_gt))
            chain(nc.vector.tensor_tensor(wide[0][:, :], wide[0][:, :], wide[1][:, :], ALU.add))
            chain(nc.vector.tensor_reduce(r3, w4[0], AX.X, ALU.add))
            chain(nc.vector.tensor_scalar(picked[:, :], rank[:, :], float(TOP), None, ALU.is_lt))
            p3 = picked[:, :].rearrange("p (n e) -> p n e", e=EXPERTS)
            chain(nc.vector.tensor_tensor(p3, p3, t["valid"][:, :].unsqueeze(2).to_broadcast([P, TILES, EXPERTS]), ALU.mult))
            dve.sem_inc(picks_ready, 1)
            m3 = masked[:, :].rearrange("p (n e) -> p n e", e=EXPERTS)
            for k in range(TOP):
                chain(nc.vector.tensor_scalar(masked[:, :], rank[:, :], float(k), None, ALU.is_equal))
                chain(nc.vector.tensor_tensor(masked[:, :], masked[:, :], logits[:, :], ALU.mult))
                chain(nc.vector.tensor_reduce(best[k][:, :], m3, AX.X, ALU.add))
            chain(nc.vector.tensor_tensor(best[1][:, :], best[1][:, :], best[0][:, :], ALU.subtract))
            dve.sem_inc(exp_ready, 1)
            dve.wait_ge(exped, 1)
            chain(nc.vector.tensor_scalar(pos[:, :], one[:, :], 1.0, None, ALU.add))
            chain(nc.vector.reciprocal(t["share0"][:, :], pos[:, :]))
            chain(nc.vector.tensor_tensor(t["share1"][:, :], t["share0"][:, :], one[:, :], ALU.mult))
            dve.wait_ge(summed, 1)
            chain(nc.vector.tensor_copy(total[:, :], psT[:, 0:TE]))
            run = scan_tiles(chain, nc, total, scan, EXPERTS)
            chain(nc.vector.tensor_copy(count[:, :], run[:, TE - EXPERTS:TE]))
            chain(nc.vector.tensor_tensor(run[:, :], run[:, :], psT[:, 0:TE], ALU.subtract))
            chain(nc.vector.tensor_tensor(run[:, :], run[:, :], psB[:, 0:TE], ALU.add))
            chain(nc.vector.tensor_scalar(full[:, :], count[:, :], float(P - 1), None, ALU.add))
            chain(nc.vector.tensor_copy(full_i[:, :], full[:, :]))
            chain(nc.vector.tensor_scalar(full_i[:, :], full_i[:, :], ~(P - 1), None, ALU.bitwise_and))
            chain(nc.vector.tensor_copy(full[:, :], full_i[:, :]))
            chain(nc.vector.memset(start[:, :], 0.0))
            for e in range(1, EXPERTS):
                chain(nc.vector.tensor_tensor(start[:, e:e + 1], start[:, e - 1:e], full[:, e - 1:e], ALU.add))
            run3 = run[:, :].rearrange("p (n e) -> p n e", e=EXPERTS)
            chain(nc.vector.tensor_tensor(run3, run3, start[:, :].unsqueeze(1).to_broadcast([P, TILES, EXPERTS]), ALU.add))
            for k in range(TOP):
                chain(nc.vector.tensor_scalar(masked[:, :], rank[:, :], float(k), None, ALU.is_equal))
                chain(nc.vector.tensor_tensor(masked[:, :], masked[:, :], run[:, :], ALU.mult))
                chain(nc.vector.tensor_reduce(pos[:, :], m3, AX.X, ALU.add))
                chain(nc.vector.tensor_tensor(pos[:, :], pos[:, :], t["valid"][:, :], ALU.mult))
                chain(nc.vector.tensor_copy(t[f"take{k}"][:, :], pos[:, :]))
                chain(nc.vector.tensor_tensor(pos[:, :], pos[:, :], t["trash"][:, :], ALU.add))
                chain(nc.vector.tensor_copy(t[f"send{k}"][:, :], pos[:, :]))
            chain(nc.vector.tensor_tensor(start[:, :], start[:, :], full[:, :], ALU.add))
            dve.wait_ge(numbered, 1)
            over3 = over[:, :].rearrange("p (n e) -> p n e", e=EXPERTS)
            shape = [1, PLACE_TILES, EXPERTS]
            chain(nc.vector.tensor_tensor(over3, start[0:1, :].unsqueeze(1).to_broadcast(shape),
                                          tile_no[:, :].unsqueeze(2).to_broadcast(shape), ALU.is_le))
            chain(nc.vector.tensor_reduce(owner[:, :], over3, AX.X, ALU.add))
            chain(nc.vector.tensor_scalar(owner[:, :], owner[:, :], float(EXPERTS - 1), None, ALU.min))
            chain(nc.vector.tensor_copy(t["owner"][:, :], owner[:, :]))

        @block.scalar
        def _(act):
            act.wait_ge(exp_ready, 1)
            nc.scalar.activation(one[:, :], best[1][:, :], ACT.Exp).then_inc(exped, 1)

        @block.tensor
        def _(pe):
            pe.wait_ge(picks_ready, 1)
            pe.matmul(psB[:, 0:TE], t["before"][:, :], picked[:, :], start=True, stop=True)
            pe.matmul(psT[:, 0:TE], t["ones"][:, :], picked[:, :], start=True, stop=True).then_inc(summed, 1)


def dispatch(core, t, dram, free):
    nc = core.nc
    w = Work(core, free)
    xn = [w.sb(f"dp_xn{b}", [P, D], F32) for b in range(2)]
    row = [w.sb(f"dp_row{b}", [P, 2 * D], F16) for b in range(2)]
    send = [w.sb(f"dp_send{b}", [P, TOP], I32) for b in range(2)]
    norm_done, hi_done, lo_done, sent_idx = core.sems("dp_norm_done", "dp_hi_done", "dp_lo_done", "dp_sent_idx")
    sent = core.sems("dp_sent0", "dp_sent1")
    DEPTH = 2
    with nc.Block() as block:

        @block.vector
        def _(dve):
            dve.sem_inc(norm_done, DEPTH)
            dve.sem_inc(lo_done, DEPTH)

            def norm(n, b):
                dve.wait_ge(lo_done, n + 1)
                normed(nc, xn[b][:, :], t["acc"], n, t["mean"], t["rstd"]).then_inc(norm_done, 1)

            def low(n, b):
                dve.wait_ge(hi_done, n + 1 + DEPTH)
                nc.vector.scalar_tensor_tensor(out=row[b][:, D:2 * D], in0=xn[b][:, :], scalar=X_SCALE, in1=row[b][:, 0:D],
                                               op0=ALU.mult, op1=ALU.subtract).then_inc(lo_done, 1)

            norm(0, 0)
            with dve.Fori(0, TILES // 2 - 1) as i:
                for b in range(2):
                    norm(2 * i + b + 1, 1 - b)
                    low(2 * i + b, b)
            norm(TILES - 1, 1)
            for b in range(2):
                low(TILES - 2 + b, b)

        @block.scalar
        def _(act):
            act.sem_inc(hi_done, DEPTH)
            with act.Fori(0, TILES // 2) as i:
                for b in range(2):
                    n = 2 * i + b
                    core.hold(act, "act", sent[b], 16 * TOP * i)
                    core.hold(act, "act", norm_done, n + 1 + DEPTH)
                    nc.scalar.activation(row[b][:, 0:D], xn[b][:, :], ACT.Copy, scale=X_SCALE).then_inc(hi_done, 1)

        @block.gpsimd
        def _(pool):
            with pool.Fori(0, TILES // 2) as i:
                for b in range(2):
                    n = 2 * i + b
                    core.hold(pool, "pool", sent[b], 16 * TOP * i)
                    for k in range(TOP):
                        pool.tensor_copy(send[b][:, k:k + 1], col(t[f"send{k}"], n)).then_inc(sent_idx, 1)
                    core.hold(pool, "pool", sent_idx, TOP * (n + 1))
                    core.hold(pool, "pool", lo_done, n + 1 + DEPTH)
                    for k in range(TOP):
                        core.hold(pool, "pool", *((sent[b], 16 * (TOP * i + k)) if k else (sent[1 - b], 16 * TOP * (i + b))))
                        pool.indirect_dma_start(out=dram["places"], out_offset=bass.IndirectOffsetOnAxis(ap=send[b][:, k:k + 1], axis=0),
                                                in_=row[b][:, :], in_offset=None).then_inc(sent[b], 16)
            for b in range(2):
                pool.wait_ge(sent[b], 16 * TOP * (TILES // 2))


def experts(core, t, dram, free, w1, w2, b1, b2):
    nc = core.nc
    w = Work(core, free)
    pair = lambda name, cols, dt: [w.sb(f"ex_{name}{b}", [P, cols], dt) for b in range(2)]
    xin, xT, g, ghi, glo, y = pair("xin", 2 * D, F16), pair("xT", 2 * D, F16), pair("g", H, F32), pair("ghi", H, F16), pair("glo", H, F16), pair("y", D, F32)
    turned, xT_done, up_done, gelu_done, ghi_done, glo_done, down_done, y_done = core.sems(
        "ex_turned", "ex_xT_done", "ex_up_done", "ex_gelu_done", "ex_ghi_done", "ex_glo_done", "ex_down_done", "ex_y_done")
    x_in, y_out = core.sems("ex_x_in0", "ex_x_in1"), core.sems("ex_y_out0", "ex_y_out1")
    psT, psY = core.bank[0:2], core.bank[6:8]
    psH = [core.bank[2:4], core.bank[4:6]]
    DEPTH = 2
    N = PLACE_TILES

    def slots(eng, slot):
        with eng.Fori(0, N // 2 - 1) as i:
            for b in range(2):
                slot(2 * i + b, b, N)
        slot(N - 2, 0, 2)
        slot(N - 1, 1, 1)

    def owner(eng, n):
        at = t["owner"][0:1, n:n + 1] if isinstance(n, int) else t["owner"][0:1, bass.ds(n, 1)]
        return eng.value_load(at, min_val=0, max_val=EXPERTS - 1)

    with nc.Block() as block:

        @block.sync
        def _(sp):
            def load(n, b):
                sp.wait_ge(turned, n + 1)
                rows = dram["places"][n * P:(n + 1) * P, :] if isinstance(n, int) else dram["places"][bass.ds(n * P, P), :]
                sp.dma_start(xin[b][:, :], rows).then_inc(x_in[b], 16)

            def store(n, b):
                sp.wait_ge(y_done, n + 1 + DEPTH)
                rows = dram["results"][n * P:(n + 1) * P, :] if isinstance(n, int) else dram["results"][bass.ds(n * P, P), :]
                sp.dma_start(rows, y[b][:, :]).then_inc(y_out[b], 16)

            def slot(n, b, left):
                if left > 2:
                    load(n + 2, b)
                store(n, b)

            for n in range(2):
                load(n, n)
            slots(sp, slot)
            for b in range(2):
                sp.wait_ge(y_out[b], 16 * (N // 2))

        @block.vector
        def _(dve):
            dve.sem_inc(glo_done, DEPTH)
            dve.sem_inc(y_done, DEPTH)

            def glow(n, b):
                dve.wait_ge(ghi_done, n + 1 + DEPTH)
                nc.vector.scalar_tensor_tensor(out=glo[b][:, :], in0=g[b][:, :], scalar=H_SCALE, in1=ghi[b][:, :],
                                               op0=ALU.mult, op1=ALU.subtract).then_inc(glo_done, 1)

            def result(n, b):
                e = owner(dve, n)
                dve.wait_ge(down_done, n + 1 + DEPTH)
                core.hold(dve, "dve", y_out[b], (n - b) * 8)
                nc.vector.scalar_tensor_tensor(out=y[b][:, :], in0=psY[b][:, 0:D], scalar=1.0 / (H_SCALE * W_SCALE),
                                               in1=b2[:, bass.ds(e * D, D)], op0=ALU.mult, op1=ALU.add).then_inc(y_done, 1)

            def slot(n, b, left):
                glow(n, b)
                result(n, b)

            slots(dve, slot)

        @block.gpsimd
        def _(pool):
            pool.sem_inc(ghi_done, DEPTH)

            def slot(n, b, left):
                core.hold(pool, "pool", glo_done, n + 1)
                core.hold(pool, "pool", down_done, n + 1)
                core.hold(pool, "pool", gelu_done, n + 1 + DEPTH)
                nc.gpsimd.tensor_scalar(ghi[b][:, :], g[b][:, :], H_SCALE, None, ALU.mult).then_inc(ghi_done, 1)

            slots(pool, slot)

        @block.scalar
        def _(act):
            act.sem_inc(xT_done, DEPTH)
            act.sem_inc(gelu_done, DEPTH)

            def copy(n, b):
                core.hold(act, "act", up_done, n + 1)
                core.hold(act, "act", turned, n + 1 + DEPTH)
                nc.scalar.activation(xT[b][:, :], psT[b][:, 0:D].bitcast(F16), ACT.Copy).then_inc(xT_done, 1)

            def gelu(n, b):
                e = owner(act, n)
                core.hold(act, "act", glo_done, n + 1)
                core.hold(act, "act", up_done, n + 1 + DEPTH)
                for c in range(HC):
                    last = nc.scalar.activation(g[b][:, c * P:(c + 1) * P], psH[b][c // 4][:, (c % 4) * P:(c % 4 + 1) * P],
                                                ACT.Gelu, bias=b1[:, bass.ds(e * HC + c, 1)], scale=1.0 / (X_SCALE * W_SCALE))
                last.then_inc(gelu_done, 1)

            def slot(n, b, left):
                if left > 2:
                    copy(n + 2, b)
                if left > 1:
                    gelu(n + 1, 1 - b)

            for n in range(2):
                copy(n, n)
            gelu(0, 0)
            slots(act, slot)

        @block.tensor
        def _(pe):
            for s in (turned, up_done, down_done):
                pe.sem_inc(s, DEPTH)

            def turn(n, b):
                pe.wait_ge(xT_done, n + 1)
                pe.wait_ge(x_in[b], (n - b) * 8 + 16)
                for c in range(2 * KC):
                    last = pe.transpose(psT[b][:, c * P // 2:(c + 1) * P // 2].bitcast(F16), xin[b][:, c * P:(c + 1) * P], t["ident16"][:, :])
                last.then_inc(turned, 1)

            def up(n, b):
                e = owner(pe, n)
                pe.wait_ge(gelu_done, n + 1)
                pe.wait_ge(xT_done, n + 1 + DEPTH)
                for c in range(HC):
                    out = psH[b][c // 4][:, (c % 4) * P:(c % 4 + 1) * P]
                    for k in range(KC):
                        whi, wlo = (w1[j][:, bass.ds(e * KC * H + (k * H + c * P), P)] for j in range(2))
                        hi, lo = (xT[b][:, (j * KC + k) * P:(j * KC + k + 1) * P] for j in range(2))
                        pe.matmul(out, whi, hi, start=k == 0, stop=False)
                        pe.matmul(out, whi, lo, start=False, stop=False)
                        last = pe.matmul(out, wlo, hi, start=False, stop=k == KC - 1)
                last.then_inc(up_done, 1)

            def down(n, b):
                e = owner(pe, n)
                pe.wait_ge(y_done, n + 1)
                pe.wait_ge(glo_done, n + 1 + DEPTH)
                for c in range(HC):
                    hi, lo = ghi[b][:, c * P:(c + 1) * P], glo[b][:, c * P:(c + 1) * P]
                    whi, wlo = (w2[j][:, bass.ds(e * HC * D + c * D, D)] for j in range(2))
                    pe.matmul(psY[b][:, 0:D], hi, whi, start=c == 0, stop=False)
                    pe.matmul(psY[b][:, 0:D], hi, wlo, start=False, stop=False)
                    last = pe.matmul(psY[b][:, 0:D], lo, whi, start=False, stop=c == HC - 1)
                last.then_inc(down_done, 1)

            def slot(n, b, left):
                if left > 2:
                    turn(n + 2, b)
                if left > 1:
                    up(n + 1, 1 - b)
                down(n, b)

            for n in range(2):
                turn(n, n)
            up(0, 0)
            slots(pe, slot)


def combine(core, t, dram, free, out):
    nc = core.nc
    w = Work(core, free)
    pair = lambda name, cols, dt: [w.sb(f"co_{name}{b}", [P, cols], dt) for b in range(2)]
    x3, half, done, take = pair("x3", D, F32), pair("half", D, F32), pair("done", D, F32), pair("take", TOP, I32)
    y = [pair(f"y{k}_", D, F32) for k in range(TOP)]
    idx_done, half_done, sum_done = core.sems("co_idx_done", "co_half_done", "co_sum_done")
    x_in, y_in, stored = core.sems("co_x_in0", "co_x_in1"), core.sems("co_y_in0", "co_y_in1"), core.sems("co_stored0", "co_stored1")
    DEPTH = 2
    with nc.Block() as block:

        @block.gpsimd
        def _(pool):
            with pool.Fori(0, TILES // 2) as i:
                for b in range(2):
                    n = 2 * i + b
                    core.hold(pool, "pool", sum_done, n + 1)
                    for k in range(TOP):
                        pool.tensor_copy(take[b][:, k:k + 1], col(t[f"take{k}"], n)).then_inc(idx_done, 1)
                    core.hold(pool, "pool", idx_done, TOP * (n + 1))
                    for k in range(TOP):
                        pool.indirect_dma_start(out=y[k][b][:, :], out_offset=None, in_=dram["results"],
                                                in_offset=bass.IndirectOffsetOnAxis(ap=take[b][:, k:k + 1], axis=0)).then_inc(y_in[b], 16)

        @block.sync
        def _(sp):
            with sp.Fori(0, TILES // 2) as i:
                for b in range(2):
                    n = 2 * i + b
                    sp.wait_ge(sum_done, n + 1)
                    sp.dma_start(x3[b][:, :], dram["x3"][bass.ds(n * P, P), :]).then_inc(x_in[b], 16)

        @block.vector
        def _(dve):
            dve.sem_inc(sum_done, DEPTH)
            dve.sem_inc(half_done, DEPTH)
            with dve.Fori(0, TILES // 2) as i:
                for b in range(2):
                    n = 2 * i + b
                    dve.wait_ge(sum_done, n + 1)
                    dve.wait_ge(x_in[b], 16 * (i + 1))
                    dve.wait_ge(y_in[b], 16 * TOP * (i + 1))
                    core.hold(dve, "dve", stored[b], 16 * i)
                    nc.vector.scalar_tensor_tensor(out=half[b][:, :], in0=y[0][b][:, :], scalar=col(t["share0"], n), in1=x3[b][:, :],
                                                   op0=ALU.mult, op1=ALU.add).then_inc(half_done, 1)
                    dve.wait_ge(half_done, n + 1 + DEPTH)
                    nc.vector.scalar_tensor_tensor(out=done[b][:, :], in0=y[1][b][:, :], scalar=col(t["share1"], n), in1=half[b][:, :],
                                                   op0=ALU.mult, op1=ALU.add).then_inc(sum_done, 1)

        @block.scalar
        def _(act):
            with act.Fori(0, TILES // 2) as i:
                for b in range(2):
                    n = 2 * i + b
                    core.hold(act, "act", sum_done, n + 1 + DEPTH)
                    act.dma_start(out[bass.ds(n * P, P), :], done[b][:, :]).then_inc(stored[b], 16)
            for b in range(2):
                act.wait_ge(stored[b], 16 * (TILES // 2))


def load_biases(core, dram, b1, b2):
    loaded = core.sem("biases_loaded")
    with core.nc.Block() as block:

        @block.sync
        def _(sp):
            sp.dma_start(b1[:, :], dram["b1_1"]).then_inc(loaded, 16)
            sp.dma_start(b2[:, :], dram["b2_1"].partition_broadcast(P)).then_inc(loaded, 16)
            sp.wait_ge(loaded, 32)


def program(nc, dram, out):
    with ExitStack() as ctx:
        core = Core(nc, ctx)
        t = {}
        for name, shape, dt in (
            ("ident", [P, P], F32), ("before", [P, P], F32), ("ones", [P, P], F32), ("ident16", [P, P], F16),
            ("iota16", [P, P], F16), ("part", [P, STEP_CHUNKS], F32), ("valid", [P, TILES], F32), ("trash", [P, TILES], F32),
            ("b0", [P, D], F32), ("wr", [P, D], F32), ("b2_0", [P, D], F32), ("br", [P, 1], F32), ("bg", [P, EXPERTS], F32),
            ("b1_0", [P, HC], F32), ("zeros", [P, 2 * 2 * D], F16), ("stats", [P, TILES * 6], F32),
            ("mean", [P, TILES], F32), ("rstd", [P, TILES], F32), ("router", [P, TILES], F32), ("chosen", [P, TILES], F32),
            ("share0", [P, TILES], F32), ("share1", [P, TILES], F32), ("owner", [1, PLACE_TILES], I32),
            ("take0", [P, TILES], I32), ("take1", [P, TILES], I32), ("send0", [P, TILES], I32), ("send1", [P, TILES], I32),
        ):
            t[name] = core.sb(name, shape, dt)
        core.ln_tmp = [core.sb(f"ln_{k}", [P, TILES], F32) for k in ("half", "var", "tmp")]
        experts_free = core.at
        for name, shape, dt in (
            ("acc", [P, TILES * D], F32), ("side", [P, TILES * D], F32),
            ("idx1", [P, STEP_COLS], I32), ("local", [P, STEP_COLS], F32), ("whi1", [P, STEP_COLS], F32), ("wlo1", [P, STEP_COLS], F32),
            ("win", [1, STEP_COLS], I32),
        ):
            t[name] = core.sb(name, shape, dt)
        free = core.at
        for name, shape, dt in (("idx0", [P, STEP_COLS], I32), ("whi0", [P, STEP_COLS], F32), ("wlo0", [P, STEP_COLS], F32)):
            t[name] = core.sb(name, shape, dt)
        first_free = core.at
        prepare(core, t, dram)
        moments(core, "ln0", t["acc"], t["stats"], t["mean"], t["rstd"])
        table0(core, t, dram, first_free)
        gather(core, t, dram["table0"], 0, t["acc"], first_free)

        w = Work(core, free)
        w1 = [w.sb(f"w1_0_{h}", [P, KC * H], F16) for h in ("hi", "lo")]
        w2 = [w.sb(f"w2_0_{h}", [P, HC * D], F16) for h in ("hi", "lo")]
        s = Work(core, w.at)
        stage = [s.sb(f"stage_0_{k}", [P, 2 * H], F32) for k in range(2)]
        split_weights(core, [
            (dram["w1_0"].rearrange("(c p) h -> p c h", p=P), stage[0][:, :].rearrange("p (c h) -> p c h", c=KC),
             w1[0][:, :].rearrange("p (c h) -> p c h", c=KC), w1[1][:, :].rearrange("p (c h) -> p c h", c=KC), None),
            (dram["w2_0"].rearrange("(c p) d -> p c d", p=P), stage[1][:, :].rearrange("p (c d) -> p c d", c=HC),
             w2[0][:, :].rearrange("p (c d) -> p c d", c=HC), w2[1][:, :].rearrange("p (c d) -> p c d", c=HC), None),
        ], W_SCALE, "split0")
        moments(core, "ln1", t["acc"], t["stats"], t["mean"], t["rstd"])
        ffn0(core, t, w.at, w1, w2)
        choose(core, t, free)

        w = Work(core, free)
        wrel = [w.sb(f"wrel_{h}", [P, KC * RELS * D], F16) for h in ("hi", "lo")]
        wgate = [w.sb(f"wgate_{h}", [P, KC * RELS], F16) for h in ("hi", "lo")]
        s = Work(core, w.at)
        gate_stage = s.sb("stage_gate", [P, KC * RELS], F32)
        stage = [s.sb(f"stage_1_{k}", [P, RELS * D], F32) for k in range(KC)]
        loads = [(dram["wgate"].rearrange("(c p) r -> p c r", p=P), gate_stage[:, :].rearrange("p (c r) -> p c r", c=KC),
                  wgate[0][:, :].rearrange("p (c r) -> p c r", c=KC), wgate[1][:, :].rearrange("p (c r) -> p c r", c=KC), None)]
        for c in range(KC):
            cut = slice(c * RELS * D, (c + 1) * RELS * D)
            loads.append((dram["wrel"][:, c * P:(c + 1) * P, :].rearrange("r p o -> p r o"), stage[c][:, :].rearrange("p (r o) -> p r o", o=D),
                          wrel[0][:, cut].rearrange("p (r o) -> p r o", o=D), wrel[1][:, cut].rearrange("p (r o) -> p r o", o=D), None))
        split_weights(core, loads, W_SCALE, "split1")

        def take_ffn(dve, n):
            return nc.vector.scalar_tensor_tensor(out=tile_of(t["acc"], n), in0=tile_of(t["side"], n), scalar=col(t["chosen"], n),
                                                  in1=tile_of(t["acc"], n), op0=ALU.mult, op1=ALU.add)

        moments(core, "ln2", t["acc"], t["stats"], t["mean"], t["rstd"], first=take_ffn)
        table1(core, t, dram, w.at, wrel, wgate)
        gather(core, t, dram["table1"], 1, t["side"], free)

        def take_gnn(dve, n):
            return nc.vector.scalar_tensor_tensor(out=tile_of(t["acc"], n), in0=tile_of(t["side"], n), scalar=0.0,
                                                  in1=tile_of(t["acc"], n), op0=ALU.max, op1=ALU.add)

        moments(core, "ln3", t["acc"], t["stats"], t["mean"], t["rstd"], first=take_gnn)
        w = Work(core, free)
        logits = w.sb("logits", [P, TILES * EXPERTS], F32)
        score(core, t, dram, w.at, logits)
        place(core, t, w.at, logits)
        dispatch(core, t, dram, free)

        w = Work(core, experts_free)
        w1 = [w.sb(f"w1_1_{h}", [P, EXPERTS * KC * H], F16) for h in ("hi", "lo")]
        w2 = [w.sb(f"w2_1_{h}", [P, EXPERTS * HC * D], F16) for h in ("hi", "lo")]
        b1 = w.sb("b1_1", [P, EXPERTS * HC], F32)
        b2 = w.sb("b2_1", [P, EXPERTS * D], F32)
        s = Work(core, w.at)
        stage = [s.sb(f"stage_2_{k}", [P, 2 * H], F32) for k in range(STAGES)]
        loads = []
        for e in range(EXPERTS):
            for view, c, halves in ((dram["w1_1"][e].rearrange("(c p) h -> p c h", p=P), KC, w1),
                                    (dram["w2_1"][e].rearrange("(c p) d -> p c d", p=P), HC, w2)):
                k = len(loads)
                part = lambda x, lo=0: x[:, lo:lo + 2 * H].rearrange("p (c h) -> p c h", c=c)
                loads.append((view, part(stage[k % STAGES]), part(halves[0], e * 2 * H), part(halves[1], e * 2 * H),
                              k - STAGES if k >= STAGES else None))
        split_weights(core, loads, W_SCALE, "split2")
        load_biases(core, dram, b1, b2)
        experts(core, t, dram, w.at, w1, w2, b1, b2)
        combine(core, t, dram, w.at, out)


def kernel(x, src, dst, edge_type_16, edge_weight, edge_weight1, L0_gnn_W, L0_gnn_b, L0_ffn_attention_mask, L0_ffn_wr, L0_ffn_br,
           L0_ffn_w1, L0_ffn_b1, L0_ffn_w2, L0_ffn_b2, L1_gnn_weight, L1_gnn_gate_weight, L1_ffn_Wg, L1_ffn_bg, L1_ffn_W1,
           L1_ffn_b1, L1_ffn_W2, L1_ffn_b2):
    import concourse.bacc as _bacc
    from concourse.bass_utils import run_bass_kernel_spmd as _run

    def edge_tiles(a, fill):
        a = np.asarray(a).reshape(-1)
        return np.pad(a, (0, EDGE_ROWS * P - EDGES), constant_values=fill).reshape(EDGE_ROWS, P)

    f = np.asarray
    far = WINDOWS * P
    dst_tiles = edge_tiles(dst, far)
    edges = np.concatenate([edge_tiles(src, 0), dst_tiles, edge_tiles(edge_type_16, 0),
                            edge_tiles(edge_weight, 0).view(np.int32), edge_tiles(edge_weight1, 0).view(np.int32)], axis=1)
    node = np.arange(TILES)[None, :] * P + np.arange(P)[:, None]
    arrays = {
        "x": np.pad(f(x), ((0, ROWS - NODES), (0, 0))),
        "edges": edges, "dst_last": dst_tiles[:, P - 1].reshape(1, EDGE_ROWS),
        "ident": np.eye(P, dtype=np.float32), "before": np.triu(np.ones((P, P), np.float32), 1),
        "valid": (node < NODES).astype(np.float32),
        "trash": np.where(node < NODES, 0, PLACES + np.arange(P)[:, None]).astype(np.float32),
        "w0T": f(L0_gnn_W).T, "b0": f(L0_gnn_b).reshape(1, D),
        "wr": f(L0_ffn_wr).reshape(1, D), "br": f(L0_ffn_br).reshape(1, 1),
        "w1_0": f(L0_ffn_w1), "b1_0": f(L0_ffn_b1).reshape(HC, P).T, "w2_0": f(L0_ffn_w2), "b2_0": f(L0_ffn_b2).reshape(1, D),
        "wrel": f(L1_gnn_weight), "wgate": f(L1_gnn_gate_weight).reshape(RELS, D).T,
        "wg": f(L1_ffn_Wg), "bg": f(L1_ffn_bg).reshape(1, EXPERTS),
        "w1_1": f(L1_ffn_W1), "b1_1": f(L1_ffn_b1).reshape(EXPERTS * HC, P).T,
        "w2_1": f(L1_ffn_W2), "b2_1": f(L1_ffn_b2).reshape(1, EXPERTS * D),
    }
    arrays = {k: np.ascontiguousarray(v) for k, v in arrays.items()}
    nc = _bacc.Bacc("TRN2", target_bir_lowering=False, num_devices=1)
    dram = {k: nc.dram_tensor(f"in_{k}", v.shape, mybir.dt.from_np(v.dtype), kind="ExternalInput").ap() for k, v in arrays.items()}
    dram["table0"] = nc.dram_tensor("table0", (ROWS, 2 * D), F16, kind="Internal").ap()
    dram["table1"] = nc.dram_tensor("table1", (ROWS * RELS, 2 * D), F16, kind="Internal").ap()
    dram["places"] = nc.dram_tensor("places", (PLACES + P, 2 * D), F16, kind="Internal").ap()
    dram["results"] = nc.dram_tensor("results", (PLACES, D), F32, kind="Internal").ap()
    dram["x3"] = nc.dram_tensor("x3", (ROWS, D), F32, kind="Internal").ap()
    out = nc.dram_tensor("out", (ROWS, D), F32, kind="ExternalOutput").ap()
    program(nc, dram, out)
    r = _run(nc, [{f"in_{k}": v for k, v in arrays.items()}], core_ids=[0])
    return r.results[0]["out"][:NODES]
```

```python
from contextlib import ExitStack

import numpy as np

import concourse.bass as bass
from concourse import mybir

F32 = mybir.dt.float32
F16 = mybir.dt.float16
I32 = mybir.dt.int32
ALU = mybir.AluOpType
ACT = mybir.ActivationFunctionType
AX = mybir.AxisListType

P = 128
D = 256
KC = D // P
BANK = 512
NODES = 6250
WINDOWS = -(-NODES // P)
TILES = WINDOWS + WINDOWS % 2
ROWS = TILES * P
EDGES = 100000
EDGE_TILES = -(-EDGES // P)
EDGE_ROWS = EDGE_TILES + 2
RELS = 16
H = 1024
HC = H // P
EXPERTS = 8
TOP = 2
CHOSEN = NODES // 2 - 1
EPS = 1e-5

BATCH = 8
BATCHES = 4
RING = BATCHES * BATCH
STEPS = -(-(EDGE_TILES + WINDOWS - 1) // RING) * RING
STEP_CHUNKS = -(-(STEPS + 4) // P)
STEP_COLS = STEP_CHUNKS * P
COLS = 5
WHI = (0, 3)
WLO = (1, 4)
LOCAL = 2

SUBS = 2
TOKENS = SUBS * P
PLACE_TILES = (NODES * TOP + EXPERTS * (TOKENS - 1)) // TOKENS
PLACE_TILES += PLACE_TILES % 2
PLACES = PLACE_TILES * TOKENS
PLACE_COLS = PLACES // P

X_SCALE = 2.0 ** 8
W_SCALE = 2.0 ** 10
H_SCALE = 2.0 ** 4
MSG_SCALE = 2.0 ** 6
EDGE_SCALE = 2.0 ** 12
FAR = -3.0e38
GROUP = 5
STAGES = 4


class Chain:

    def __init__(self, eng, sem, start=0):
        self.eng, self.sem, self.n = eng, sem, start

    def __call__(self, ins):
        self.n += 1
        ins.then_inc(self.sem, 1)
        self.eng.wait_ge(self.sem, self.n)


class Core:

    def __init__(self, nc, ctx):
        self.nc, self.ctx = nc, ctx
        self.at = -(-nc.sbuf_base // 64) * 64
        self.arrived = [self.sem(f"arrived{k}") for k in range(BATCHES)]
        self.held = {e: self.sem(f"{e}_held") for e in ("act", "pool", "dve")}
        self.psum = ctx.enter_context(nc.psum_tensor("psum", [P, 8 * BANK], F32))
        self.bank = [self.psum[:, i * BANK:(i + 1) * BANK] for i in range(8)]

    def sem(self, name):
        return self.ctx.enter_context(self.nc.semaphore(name))

    def sems(self, *names):
        return [self.sem(n) for n in names]

    def sb(self, name, shape, dt, at=None):
        size = int(np.prod(shape[1:])) * mybir.dt.size(dt)
        if at is None:
            at, self.at = self.at, self.at + -(-size // 64) * 64
        assert at + size <= self.nc.sbuf_usable_end, (name, at + size, self.nc.sbuf_usable_end)
        return self.nc.alloc_sbuf_tensor_at(name, shape, dt, offset=at, align_bytes=4)

    def work(self):
        return Work(self)

    def hold(self, eng, which, sem, value):
        eng.wait_ge(sem, value)
        eng.sem_inc(self.held[which], 1)


class Work:
    def __init__(self, core, at=None):
        self.core, self.at = core, core.at if at is None else at

    def sb(self, name, shape, dt):
        size = int(np.prod(shape[1:])) * mybir.dt.size(dt)
        t = self.core.sb(name, shape, dt, at=self.at)
        self.at += -(-size // 64) * 64
        return t


def split_weights(core, loads, scale, name):
    nc = core.nc
    stages = min(STAGES, len(loads))
    loaded = [core.sem(f"{name}_loaded{k}") for k in range(stages)]
    hi_done, lo_done = core.sems(f"{name}_hi_done", f"{name}_lo_done")
    with nc.Block() as block:

        @block.sync
        def _(sp):
            for k, (view, to, stage, hi, lo, before) in enumerate(loads):
                if before is not None:
                    sp.wait_ge(lo_done, before + 1)
                sp.dma_start(to, view).then_inc(loaded[k % stages], 16)

        @block.scalar
        def _(act):
            for k, (view, to, stage, hi, lo, before) in enumerate(loads):
                act.wait_ge(loaded[k % stages], 16 * (k // stages + 1))
                nc.scalar.activation(hi, stage, ACT.Copy, scale=scale).then_inc(hi_done, 1)

        @block.vector
        def _(dve):
            for k, (view, to, stage, hi, lo, before) in enumerate(loads):
                dve.wait_ge(hi_done, k + 1)
                nc.vector.scalar_tensor_tensor(out=lo, in0=stage, scalar=scale, in1=hi,
                                               op0=ALU.mult, op1=ALU.subtract).then_inc(lo_done, 1)


def tile_of(t, n, width=D):
    return t[:, n * width:(n + 1) * width] if isinstance(n, int) else t[:, bass.ds(n * width, width)]


def col(t, n):
    return t[:, n:n + 1] if isinstance(n, int) else t[:, bass.ds(n, 1)]


def moments(core, name, src, stats, mean, rstd, first=None):
    nc = core.nc
    made, link, root, rooted = core.sems(f"{name}_made", f"{name}_link", f"{name}_root", f"{name}_rooted")
    half, var, tmp = core.ln_tmp
    s6 = stats[:, :].rearrange("p (n s) -> p n s", s=6)
    groups = TILES // GROUP
    with nc.Block() as block:

        @block.vector
        def _(dve):
            def statistics(i):
                for k in range(GROUP):
                    n = i * GROUP + k
                    nc.vector.bn_stats(tile_of(stats, n, 6), tile_of(src, n)).then_inc(link, 1)

            if first is None:
                with dve.Fori(0, groups) as i:
                    statistics(i)
            else:
                first(dve, 0).then_inc(made, 1)
                with dve.Fori(0, groups - 1) as i:
                    first(dve, i + 1).then_inc(made, 1)
                    core.hold(dve, "dve", made, i + 1)
                    statistics(i)
                core.hold(dve, "dve", made, groups)
                statistics(groups - 1)
            dve.wait_ge(link, TILES)
            chain = Chain(dve, link, TILES)
            chain(nc.vector.tensor_tensor(mean[:, :], s6[:, :, 1], s6[:, :, 4], ALU.add))
            chain(nc.vector.tensor_tensor(half[:, :], s6[:, :, 1], s6[:, :, 4], ALU.subtract))
            chain(nc.vector.tensor_tensor(var[:, :], s6[:, :, 2], s6[:, :, 5], ALU.add))
            chain(nc.vector.tensor_scalar(mean[:, :], mean[:, :], 0.5, None, ALU.mult))
            chain(nc.vector.tensor_tensor(half[:, :], half[:, :], half[:, :], ALU.mult))
            chain(nc.vector.tensor_scalar(var[:, :], var[:, :], 1.0 / D, EPS, ALU.mult, ALU.add))
            chain(nc.vector.scalar_tensor_tensor(out=var[:, :], in0=half[:, :], scalar=0.25, in1=var[:, :],
                                                 op0=ALU.mult, op1=ALU.add))
            dve.sem_inc(root, 1)
            dve.wait_ge(rooted, 1)
            chain(nc.vector.reciprocal(rstd[:, :], tmp[:, :]))
            chain(nc.vector.tensor_tensor(tmp[:, :], rstd[:, :], rstd[:, :], ALU.mult))
            chain(nc.vector.tensor_tensor(tmp[:, :], tmp[:, :], var[:, :], ALU.mult))
            chain(nc.vector.tensor_scalar(tmp[:, :], tmp[:, :], -0.5, 1.5, ALU.mult, ALU.add))
            chain(nc.vector.tensor_tensor(rstd[:, :], rstd[:, :], tmp[:, :], ALU.mult))

        @block.scalar
        def _(act):
            act.wait_ge(root, 1)
            nc.scalar.activation(tmp[:, :], var[:, :], ACT.Sqrt).then_inc(rooted, 1)


def normed(nc, out, src, n, mean, rstd):
    return nc.vector.tensor_scalar(out, tile_of(src, n), col(mean, n), col(rstd, n), ALU.subtract, ALU.mult)


def prepare(core, t, dram):
    nc = core.nc
    w = Work(core)
    last = w.sb("last_dst", [WINDOWS - 1, EDGE_ROWS], I32)
    before = w.sb("before_window", [WINDOWS - 1, EDGE_ROWS], F32)
    ends = w.sb("window_ends", [WINDOWS - 1, 1], F32)
    step_no = w.sb("step_no", [P, STEP_COLS], F32)
    passed = w.sb("windows_passed", [WINDOWS - 1, STEP_COLS], F32)
    win_col = w.sb("win_col", [P, STEP_CHUNKS], F32)
    tile_col = w.sb("tile_col", [P, STEP_CHUNKS], F32)
    tile_idx = w.sb("tile_idx", [P, STEP_CHUNKS], I32)
    low_col = w.sb("low_col", [P, STEP_CHUNKS], F32)
    edges = w.sb("step_edges", [P, STEP_CHUNKS * 5 * P], I32)
    cols = w.sb("step_cols", [P, STEP_CHUNKS * 5 * P], F32)
    half = [w.sb(f"weight_half{g}", [P, STEP_COLS], F16) for g in range(2)]
    loaded, x_loaded, iotad, link, steps_known, gathered, ready, turned, emptied, made0 = core.sems(
        "consts_loaded", "x_loaded", "iota_made", "prep_link", "steps_known", "edges_gathered",
        "cols_ready", "cols_turned", "cols_emptied", "zeros_made")
    win_ready = core.sem("win_ready")
    per = 10
    step_cols = t["step_cols"][:, :].rearrange("p (s f) -> p s f", f=COLS)
    with nc.Block() as block:

        @block.sync
        def _(sp):
            sp.dma_start(last[:, :], dram["dst_last"].partition_broadcast(WINDOWS - 1)).then_inc(loaded, 16)
            sp.dma_start(t["ident"][:, :], dram["ident"]).then_inc(loaded, 16)
            sp.dma_start(t["before"][:, :], dram["before"]).then_inc(loaded, 16)
            sp.dma_start(t["valid"][:, :], dram["valid"]).then_inc(loaded, 16)
            for name in ("b0", "wr", "b2_0"):
                sp.dma_start(t[name][:, :], dram[name].partition_broadcast(P)).then_inc(loaded, 16)
            sp.dma_start(t["br"][:, :], dram["br"].partition_broadcast(P)).then_inc(loaded, 16)
            sp.dma_start(t["bg"][:, :], dram["bg"].partition_broadcast(P)).then_inc(loaded, 16)
            sp.dma_start(t["b1_0"][:, :], dram["b1_0"]).then_inc(loaded, 16)
            acc = t["acc"][:, :].rearrange("p (n d) -> p n d", d=D)
            for k in range(TILES // per):
                rows = dram["x"][k * per * P:(k + 1) * per * P, :]
                sp.dma_start(acc[:, k * per:(k + 1) * per, :], rows.rearrange("(n p) d -> p n d", p=P)).then_inc(x_loaded, 16)
            sp.wait_ge(x_loaded, 16 * (TILES // per))

        @block.gpsimd
        def _(pool):
            pool.iota(step_no[:, :], pattern=[[1, STEP_COLS]], base=0, channel_multiplier=0,
                      allow_small_or_imprecise_dtypes=True).then_inc(iotad, 1)
            pool.iota(t["part"][:, :], pattern=[[P, STEP_CHUNKS]], base=0, channel_multiplier=1,
                      allow_small_or_imprecise_dtypes=True).then_inc(iotad, 1)
            pool.memset(t["side"][:, WINDOWS * D:], 0.0).then_inc(made0, 1)
            pool.wait_ge(made0, 1)
            pool.wait_ge(steps_known, 1)
            for k in range(STEP_CHUNKS):
                pool.indirect_dma_start(
                    out=edges[:, k * 5 * P:(k + 1) * 5 * P], out_offset=None, in_=dram["edges"],
                    in_offset=bass.IndirectOffsetOnAxis(ap=tile_idx[:, k:k + 1], axis=0)).then_inc(gathered, 16)

        @block.vector
        def _(dve):
            chain = Chain(dve, link)
            chain(nc.vector.memset(t["ones"][:, :], 1.0))
            dve.wait_ge(iotad, 2)
            dve.wait_ge(loaded, 16 * 10)
            chain(nc.vector.tensor_copy(t["ident16"][:, :], t["ident"][:, :]))
            chain(nc.vector.tensor_copy(t["iota16"][:, :], step_no[:, 0:P]))
            chain(nc.vector.tensor_scalar(ends[:, :], t["part"][0:WINDOWS - 1, 0:1], 128.0, 128.0, ALU.mult, ALU.add))
            chain(nc.vector.tensor_scalar(before[:, :], last[:, :], ends[:, :], None, ALU.is_lt))
            chain(nc.vector.tensor_reduce(ends[:, :], before[:, :], AX.X, ALU.add))
            chain(nc.vector.tensor_tensor(ends[:, :], ends[:, :], t["part"][0:WINDOWS - 1, 0:1], ALU.add))
            chain(nc.vector.memset(t["last_step"][:, :], STEPS - 1))
            chain(nc.vector.tensor_scalar(passed[:, :], step_no[0:WINDOWS - 1, :], ends[:, :], None, ALU.is_gt))
            dve.sem_inc(ready, 1)
            dve.wait_ge(turned, 1)
            chain(nc.vector.tensor_copy(win_col[:, :], core.bank[0][:, 0:STEP_CHUNKS]))
            for k in range(2):
                chain(nc.vector.tensor_copy(t["win"][0:1, k * (STEP_COLS // 2):(k + 1) * (STEP_COLS // 2)],
                                            core.bank[1 + k][0:1, 0:STEP_COLS // 2]))
            chain(nc.vector.tensor_copy(t["last_step"][0:1, 0:WINDOWS - 1], core.bank[3][0:1, 0:WINDOWS - 1]))
            chain(nc.vector.tensor_tensor(tile_col[:, :], t["part"][:, :], win_col[:, :], ALU.subtract))
            chain(nc.vector.tensor_scalar(tile_col[:, :], tile_col[:, :], float(EDGE_ROWS - 1), None, ALU.min))
            chain(nc.vector.tensor_scalar(low_col[:, :], win_col[:, :], float(P), None, ALU.mult))
            chain(nc.vector.tensor_copy(tile_idx[:, :], tile_col[:, :]))
            dve.sem_inc(steps_known, 1)
            dve.wait_ge(gathered, 16 * STEP_CHUNKS)
            e = edges[:, :].rearrange("p (k f e) -> p k f e", f=5, e=P)
            c = cols[:, :].rearrange("p (k f e) -> p k f e", f=5, e=P)
            for k in range(STEP_CHUNKS):
                chain(nc.vector.tensor_copy(c[:, k, 0, :], e[:, k, 0, :]))
                chain(nc.vector.scalar_tensor_tensor(out=c[:, k, 1, :], in0=e[:, k, 0, :], scalar=float(RELS),
                                                     in1=e[:, k, 2, :], op0=ALU.mult, op1=ALU.add))
                chain(nc.vector.tensor_scalar(c[:, k, 2, :], e[:, k, 1, :], low_col[:, k:k + 1], None, ALU.subtract))
                chain(nc.vector.tensor_scalar(c[:, k, 3:5, :], e[:, k, 3:5, :].bitcast(F32), EDGE_SCALE, None, ALU.mult))
            dve.sem_inc(ready, 1)
            for k in range(STEP_CHUNKS):
                dve.wait_ge(turned, 2 + k)
                a, b = core.bank[2 * (k % 2)], core.bank[2 * (k % 2) + 1]
                cut = slice(k * P, (k + 1) * P)
                nc.vector.tensor_copy(t["idx0"][:, cut], a[:, 0:P])
                nc.vector.tensor_copy(t["idx1"][:, cut], a[:, P:2 * P])
                nc.vector.tensor_copy(step_cols[:, cut, LOCAL], a[:, 2 * P:3 * P])
                for g, from_ in ((0, a[:, 3 * P:4 * P]), (1, b[:, 0:P])):
                    chain(nc.vector.tensor_copy(half[g][:, cut], from_))
                    chain(nc.vector.tensor_copy(step_cols[:, cut, WHI[g]], half[g][:, cut]))
                    nc.vector.tensor_tensor(step_cols[:, cut, WLO[g]], from_, half[g][:, cut], ALU.subtract).then_inc(emptied, 1)

        @block.tensor
        def _(pe):
            pe.wait_ge(ready, 1)
            for k in range(STEP_CHUNKS):
                pe.matmul(core.bank[0][:, k:k + 1], passed[:, k * P:(k + 1) * P], t["ones"][0:WINDOWS - 1, 0:1],
                          start=True, stop=True)
            for k in range(2):
                last_mm = pe.matmul(core.bank[1 + k][0:1, 0:STEP_COLS // 2], t["ones"][0:WINDOWS - 1, 0:1],
                                    passed[:, k * (STEP_COLS // 2):(k + 1) * (STEP_COLS // 2)], start=True, stop=True)
            last_mm = pe.matmul(core.bank[3][0:1, 0:WINDOWS - 1], ends[:, :], t["ident"][0:WINDOWS - 1, 0:WINDOWS - 1],
                                start=True, stop=True)
            last_mm.then_inc(turned, 1)
            pe.wait_ge(ready, 2)
            c = cols[:, :].rearrange("p (k f e) -> p k f e", f=5, e=P)
            for k in range(STEP_CHUNKS):
                if k >= 2:
                    pe.wait_ge(emptied, 2 * (k - 1))
                for f in range(5):
                    last_mm = pe.transpose(core.bank[2 * (k % 2) + f // 4][:, (f % 4) * P:(f % 4 + 1) * P],
                                           c[:, k, f, :], t["ident"][:, :])
                last_mm.then_inc(turned, 1)


def table0(core, t, dram, weights):
    nc = core.nc
    w = Work(core, weights)
    xn = [w.sb(f"t0_xn{b}", [P, D], F32) for b in range(2)]
    xT = [w.sb(f"t0_xT{b}", [P, D], F32) for b in range(2)]
    row = [w.sb(f"t0_row{b}", [P, 2 * D], F16) for b in range(2)]
    w0 = w.sb("t0_w0", [P, KC * D], F32)
    loaded, norm_done, turn_done, xT_done, mm_done, hi_done, lo_done, bias_done = core.sems(
        "t0_loaded", "t0_norm_done", "t0_turn_done", "t0_xT_done", "t0_mm_done", "t0_hi_done", "t0_lo_done", "t0_bias_done")
    stored = core.sems("t0_stored0", "t0_stored1")
    psT, psY = core.bank[0:2], core.bank[2:4]
    DEPTH = 2
    tab = dram["table0"].rearrange("(n p) d -> n p d", p=P)
    with nc.Block() as block:

        @block.sync
        def _(sp):
            for b in range(2):
                sp.sem_inc(stored[b], 16)
            sp.dma_start(w0[:, :].rearrange("p (c o) -> p c o", c=KC), dram["w0T"].rearrange("(c p) o -> p c o", p=P)).then_inc(loaded, 16)
            with sp.Fori(0, TILES // 2) as i:
                for b in range(2):
                    n = 2 * i + b
                    sp.wait_ge(lo_done, n + 1 + DEPTH)
                    sp.dma_start(dram["table0"][bass.ds(n * P, P), :], row[b][:, :]).then_inc(stored[b], 16)
            for b in range(2):
                sp.wait_ge(stored[b], 16 * (TILES // 2) + 16)

        @block.vector
        def _(dve):
            dve.sem_inc(norm_done, DEPTH)
            dve.sem_inc(lo_done, DEPTH)

            def norm(n, b):
                dve.wait_ge(turn_done, n + 1)
                normed(nc, xn[b][:, :], t["acc"], n, t["mean"], t["rstd"]).then_inc(norm_done, 1)

            def low(n, b):
                dve.wait_ge(hi_done, n + 1 + DEPTH)
                nc.vector.scalar_tensor_tensor(out=row[b][:, D:2 * D], in0=psY[b][:, 0:D], scalar=MSG_SCALE,
                                               in1=row[b][:, 0:D], op0=ALU.mult, op1=ALU.subtract).then_inc(lo_done, 1)

            for b in range(2):
                norm(b, b)
            with dve.Fori(0, TILES // 2 - 1) as i:
                for b in range(2):
                    norm(2 * i + 2 + b, b)
                    low(2 * i + b, b)
            for b in range(2):
                low(TILES - 2 + b, b)

        @block.gpsimd
        def _(pool):
            with pool.Fori(0, TILES) as n:
                core.hold(pool, "pool", norm_done, n + 1 + DEPTH)
                nc.gpsimd.tensor_tensor(tile_of(t["acc"], n), tile_of(t["acc"], n), t["b0"][:, :], ALU.add).then_inc(bias_done, 1)
            pool.wait_ge(bias_done, TILES)

        @block.tensor
        def _(pe):
            pe.sem_inc(turn_done, DEPTH)
            pe.sem_inc(mm_done, DEPTH)
            pe.wait_ge(loaded, 16)

            def turn(n, b):
                pe.wait_ge(norm_done, n + 1 + DEPTH)
                pe.wait_ge(xT_done, n + 1)
                for c in range(KC):
                    last = pe.transpose(psT[b][:, c * P:(c + 1) * P], xn[b][:, c * P:(c + 1) * P], t["ident"][:, :])
                last.then_inc(turn_done, 1)

            def product(n, b):
                pe.wait_ge(xT_done, n + 1 + DEPTH)
                pe.wait_ge(lo_done, n + 1)
                for c in range(KC):
                    last = pe.matmul(psY[b][:, 0:D], xT[b][:, c * P:(c + 1) * P], w0[:, c * D:(c + 1) * D],
                                     start=c == 0, stop=c == KC - 1)
                last.then_inc(mm_done, 1)

            for b in range(2):
                turn(b, b)
            with pe.Fori(0, TILES // 2 - 1) as i:
                for b in range(2):
                    product(2 * i + b, b)
                    turn(2 * i + 2 + b, b)
            for b in range(2):
                product(TILES - 2 + b, b)

        @block.scalar
        def _(act):
            act.sem_inc(xT_done, DEPTH)
            act.sem_inc(hi_done, DEPTH)

            def copy(n, b):
                act.wait_ge(turn_done, n + 1 + DEPTH)
                act.wait_ge(mm_done, n + 1)
                nc.scalar.activation(xT[b][:, :], psT[b][:, 0:D], ACT.Copy).then_inc(xT_done, 1)

            def high(n, b):
                act.wait_ge(mm_done, n + 1 + DEPTH)
                core.hold(act, "act", stored[b], (n - b) * 8 + 16)
                nc.scalar.activation(row[b][:, 0:D], psY[b][:, 0:D], ACT.Copy, scale=MSG_SCALE).then_inc(hi_done, 1)

            for b in range(2):
                copy(b, b)
            with act.Fori(0, TILES // 2 - 1) as i:
                for b in range(2):
                    high(2 * i + b, b)
                    copy(2 * i + 2 + b, b)
            for b in range(2):
                high(TILES - 2 + b, b)


def gather(core, t, table, g, out, weights):
    nc = core.nc
    w = Work(core, weights)
    name = f"g{g}"
    rounds = STEPS // RING
    msg = [w.sb(f"{name}_msg{k}", [P, 2 * D], F16) for k in range(RING)]
    idx = [w.sb(f"{name}_idx{b}", [P, BATCH], I32) for b in range(BATCHES)]
    PAIR = 2
    cols = [w.sb(f"{name}_cols{b}", [P, BATCH * 3], F32) for b in range(PAIR)]
    hot = [w.sb(f"{name}_hot{b}", [P, BATCH * 2 * P], F16) for b in range(PAIR)]
    zeros = w.sb(f"{name}_zeros", [P, D], F32)
    arrived, before = core.arrived, g * rounds * BATCH * 16
    idx_done, cols_done, hot_done, mm_done, bank_free, copied, zeroed = core.sems(*(
        f"{name}_{k}" for k in ("idx_done", "cols_done", "hot_done", "mm_done", "bank_free", "copied", "zeroed")))
    BANKS = 4
    first = min(WHI[g], LOCAL)
    scale = 1.0 / (MSG_SCALE * EDGE_SCALE)
    with nc.Block() as block:

        @block.gpsimd
        def _(pool):
            pool.memset(zeros[:, :], 0.0).then_inc(zeroed, 1)
            with pool.Fori(0, rounds) as i:
                for b in range(BATCHES):
                    m = BATCHES * i + b
                    core.hold(pool, "pool", mm_done, m * BATCH + BATCH)
                    pool.tensor_copy(idx[b][:, :], t[f"idx{g}"][:, bass.ds(m * BATCH, BATCH)]).then_inc(idx_done, 1)
                    core.hold(pool, "pool", idx_done, m + 1)
                    for k in range(BATCH):
                        pool.indirect_dma_start(
                            out=msg[b * BATCH + k][:, :], out_offset=None, in_=table,
                            in_offset=bass.IndirectOffsetOnAxis(ap=idx[b][:, k:k + 1], axis=0)).then_inc(arrived[b], 16)

        @block.vector
        def _(dve):
            dve.sem_inc(hot_done, PAIR)
            with dve.Fori(0, STEPS // BATCH // PAIR) as i:
                for b in range(PAIR):
                    m = PAIR * i + b
                    c3 = cols[b][:, :].rearrange("p (s f) -> p s f", f=3)
                    core.hold(dve, "dve", mm_done, m * BATCH + BATCH + RING - PAIR * BATCH)
                    steps = t["step_cols"][:, bass.ds(m * BATCH * COLS, BATCH * COLS)].rearrange("p (s f) -> p s f", f=COLS)
                    nc.vector.tensor_copy(c3, steps[:, :, first:first + 3]).then_inc(cols_done, 1)
                    core.hold(dve, "dve", cols_done, m + 1)
                    for k in range(BATCH):
                        for h, half in enumerate((WHI[g], WLO[g])):
                            last = nc.vector.tensor_scalar(
                                hot[b][:, (2 * k + h) * P:(2 * k + h + 1) * P], t["iota16"][:, :],
                                c3[:, k, LOCAL - first:LOCAL - first + 1], c3[:, k, half - first:half - first + 1],
                                ALU.is_equal, ALU.mult)
                    last.then_inc(hot_done, 1)

        @block.tensor
        def _(pe):
            pe.sem_inc(mm_done, RING)
            with pe.Fori(0, rounds) as i:
                for b in range(BATCHES):
                    m = BATCHES * i + b
                    pe.wait_ge(hot_done, m + 1 + PAIR)
                    pe.wait_ge(arrived[b], before + 16 * BATCH * (i + 1))
                    for k in range(BATCH):
                        s = m * BATCH + k
                        at = pe.value_load(t["win"][0:1, bass.ds(s, 1)], min_val=0, max_val=WINDOWS - 1)
                        pe.wait_ge(bank_free, at + 1)
                        ps = core.psum[:, bass.ds((at % BANKS) * BANK, D)]
                        hi, lo = (hot[b % PAIR][:, (2 * k + h) * P:(2 * k + h + 1) * P] for h in range(2))
                        row = msg[b * BATCH + k]
                        pe.matmul(ps, hi, row[:, 0:D], start=False, stop=False, skip_group_check=True)
                        pe.matmul(ps, hi, row[:, D:2 * D], start=False, stop=False, skip_group_check=True)
                        pe.matmul(ps, lo, row[:, 0:D], start=False, stop=False, skip_group_check=True).then_inc(mm_done, 1)

        @block.scalar
        def _(act):
            def clear(b):
                nc.scalar.activation(core.bank[b][:, 0:D], zeros[:, :], ACT.Copy).then_inc(bank_free, 1)

            def window(n, b):
                at = t["last_step"][0:1, n:n + 1] if isinstance(n, int) else t["last_step"][0:1, bass.ds(n, 1)]
                last = act.value_load(at, min_val=0, max_val=STEPS - 1)
                core.hold(act, "act", mm_done, last + 1 + RING)
                nc.scalar.activation(tile_of(out, n), core.bank[b][:, 0:D], ACT.Copy, scale=scale).then_inc(copied, 1)

            act.wait_ge(zeroed, 1)
            for b in range(BANKS):
                clear(b)
            with act.Fori(0, WINDOWS // BANKS) as i:
                for b in range(BANKS):
                    window(BANKS * i + b, b)
                    act.wait_ge(copied, BANKS * i + b + 1)
                    clear(b)
            for n in range(WINDOWS // BANKS * BANKS, WINDOWS):
                window(n, n % BANKS)
            act.wait_ge(copied, WINDOWS)


def ffn0(core, t, free, w1, w2):
    nc = core.nc
    w = Work(core, free)
    pair = lambda name, cols, dt: [w.sb(f"f0_{name}{b}", [P, cols], dt) for b in range(2)]
    xn, junk, dot = pair("xn", D, F32), pair("junk", D, F32), pair("dot", 1, F32)
    xhi, xlo = pair("xhi", D, F16), pair("xlo", D, F16)
    g, ghi, glo = pair("g", H, F32), pair("ghi", H, F16), pair("glo", H, F16)
    norm_done, dot_done, routed, added, turned, xhi_done, xlo_done, up_done, gelu_done, ghi_done, glo_done, down_done, out_done = core.sems(
        "f0_norm_done", "f0_dot_done", "f0_routed", "f0_added", "f0_turned", "f0_xhi_done", "f0_xlo_done", "f0_up_done", "f0_gelu_done",
        "f0_ghi_done", "f0_glo_done", "f0_down_done", "f0_out_done")
    psT, psY = core.bank[0:2], core.bank[6:8]
    psH = [core.bank[2:4], core.bank[4:6]]
    DEPTH = 2
    LEAD = 3

    def slots(eng, slot):
        body = TILES - LEAD - (TILES - LEAD) % 2
        with eng.Fori(0, body // 2) as i:
            for b in range(2):
                slot(2 * i + b, b, TILES)
        for n in range(body, TILES):
            slot(n, n % 2, TILES - n)

    with nc.Block() as block:

        @block.vector
        def _(dve):
            for s in (norm_done, dot_done, routed, xlo_done, glo_done, out_done):
                dve.sem_inc(s, DEPTH)

            def norm(n, b):
                dve.wait_ge(turned, n + 1)
                dve.wait_ge(added, n + 1)
                dve.wait_ge(dot_done, n + 1)
                normed(nc, xn[b][:, :], t["acc"], n, t["mean"], t["rstd"]).then_inc(norm_done, 1)

            def route(n, b):
                dve.wait_ge(norm_done, n + 1 + DEPTH)
                dve.wait_ge(routed, n + 1)
                nc.vector.tensor_tensor_reduce(out=junk[b][:, :], in0=xn[b][:, :], in1=t["wr"][:, :], scale=1.0, scalar=0.0,
                                               op0=ALU.mult, op1=ALU.add, accum_out=dot[b][:, :]).then_inc(dot_done, 1)
                dve.wait_ge(dot_done, n + 1 + DEPTH)
                nc.vector.tensor_scalar(col(t["router"], n), dot[b][:, :], t["br"][:, :], None, ALU.add).then_inc(routed, 1)

            def xlow(n, b):
                dve.wait_ge(xhi_done, n + 1 + DEPTH)
                nc.vector.scalar_tensor_tensor(out=xlo[b][:, :], in0=psT[b][:, 0:D], scalar=X_SCALE, in1=xhi[b][:, :],
                                               op0=ALU.mult, op1=ALU.subtract).then_inc(xlo_done, 1)

            def glow(n, b):
                dve.wait_ge(ghi_done, n + 1 + DEPTH)
                nc.vector.scalar_tensor_tensor(out=glo[b][:, :], in0=g[b][:, :], scalar=H_SCALE, in1=ghi[b][:, :],
                                               op0=ALU.mult, op1=ALU.subtract).then_inc(glo_done, 1)

            def result(n, b):
                dve.wait_ge(down_done, n + 1 + DEPTH)
                nc.vector.scalar_tensor_tensor(out=tile_of(t["side"], n), in0=psY[b][:, 0:D], scalar=1.0 / (H_SCALE * W_SCALE),
                                               in1=t["b2_0"][:, :], op0=ALU.mult, op1=ALU.add).then_inc(out_done, 1)

            def slot(n, b, left):
                if left > 3:
                    norm(n + 3, 1 - b)
                glow(n, b)
                if left > 2:
                    xlow(n + 2, b)
                if left > 3:
                    route(n + 3, 1 - b)
                result(n, b)

            for n in range(2):
                norm(n, n)
                route(n, n)
            for n in range(2):
                xlow(n, n)
            norm(2, 0)
            route(2, 0)
            slots(dve, slot)

        @block.gpsimd
        def _(pool):
            pool.sem_inc(added, DEPTH)
            pool.sem_inc(ghi_done, DEPTH)

            def add(n, b):
                core.hold(pool, "pool", norm_done, n + 1 + DEPTH)
                nc.gpsimd.tensor_tensor(tile_of(t["acc"], n), tile_of(t["acc"], n), xn[b][:, :], ALU.add).then_inc(added, 1)

            def ghigh(n, b):
                core.hold(pool, "pool", glo_done, n + 1)
                core.hold(pool, "pool", down_done, n + 1)
                core.hold(pool, "pool", gelu_done, n + 1 + DEPTH)
                nc.gpsimd.tensor_scalar(ghi[b][:, :], g[b][:, :], H_SCALE, None, ALU.mult).then_inc(ghi_done, 1)

            def slot(n, b, left):
                ghigh(n, b)
                if left > 2:
                    add(n + 2, b)

            for n in range(2):
                add(n, n)
            slots(pool, slot)

        @block.scalar
        def _(act):
            act.sem_inc(xhi_done, DEPTH)
            act.sem_inc(gelu_done, DEPTH)

            def xhigh(n, b):
                core.hold(act, "act", up_done, n + 1)
                core.hold(act, "act", turned, n + 1 + DEPTH)
                nc.scalar.activation(xhi[b][:, :], psT[b][:, 0:D], ACT.Copy, scale=X_SCALE).then_inc(xhi_done, 1)

            def gelu(n, b):
                core.hold(act, "act", glo_done, n + 1)
                core.hold(act, "act", up_done, n + 1 + DEPTH)
                for c in range(HC):
                    last = nc.scalar.activation(g[b][:, c * P:(c + 1) * P], psH[b][c // 4][:, (c % 4) * P:(c % 4 + 1) * P],
                                                ACT.Gelu_apprx_tanh, bias=t["b1_0"][:, c:c + 1], scale=1.0 / (X_SCALE * W_SCALE))
                last.then_inc(gelu_done, 1)

            def slot(n, b, left):
                if left > 2:
                    xhigh(n + 2, b)
                if left > 1:
                    gelu(n + 1, 1 - b)

            for n in range(2):
                xhigh(n, n)
            gelu(0, 0)
            slots(act, slot)

        @block.tensor
        def _(pe):
            for s in (turned, up_done, down_done):
                pe.sem_inc(s, DEPTH)

            def turn(n, b):
                pe.wait_ge(xlo_done, n + 1)
                pe.wait_ge(norm_done, n + 1 + DEPTH)
                for c in range(KC):
                    last = pe.transpose(psT[b][:, c * P:(c + 1) * P], xn[b][:, c * P:(c + 1) * P], t["ident"][:, :])
                last.then_inc(turned, 1)

            def up(n, b):
                pe.wait_ge(gelu_done, n + 1)
                pe.wait_ge(xlo_done, n + 1 + DEPTH)
                for c in range(HC):
                    out = psH[b][c // 4][:, (c % 4) * P:(c % 4 + 1) * P]
                    for k in range(KC):
                        whi, wlo = (w1[j][:, k * H + c * P:k * H + (c + 1) * P] for j in range(2))
                        hi, lo = xhi[b][:, k * P:(k + 1) * P], xlo[b][:, k * P:(k + 1) * P]
                        pe.matmul(out, whi, hi, start=k == 0, stop=False)
                        pe.matmul(out, whi, lo, start=False, stop=False)
                        last = pe.matmul(out, wlo, hi, start=False, stop=k == KC - 1)
                last.then_inc(up_done, 1)

            def down(n, b):
                pe.wait_ge(out_done, n + 1)
                pe.wait_ge(glo_done, n + 1 + DEPTH)
                for c in range(HC):
                    hi, lo = ghi[b][:, c * P:(c + 1) * P], glo[b][:, c * P:(c + 1) * P]
                    whi, wlo = (w2[j][:, c * D:(c + 1) * D] for j in range(2))
                    pe.matmul(psY[b][:, 0:D], hi, whi, start=c == 0, stop=False)
                    pe.matmul(psY[b][:, 0:D], hi, wlo, start=False, stop=False)
                    last = pe.matmul(psY[b][:, 0:D], lo, whi, start=False, stop=c == HC - 1)
                last.then_inc(down_done, 1)

            def slot(n, b, left):
                if left > 2:
                    turn(n + 2, b)
                if left > 1:
                    up(n + 1, 1 - b)
                down(n, b)

            for n in range(2):
                turn(n, n)
            up(0, 0)
            slots(pe, slot)


def scan_tiles(chain, nc, a, b, width):
    step = 1
    while step < TILES:
        chain(nc.vector.tensor_copy(b[:, 0:step * width], a[:, 0:step * width]))
        chain(nc.vector.tensor_tensor(b[:, step * width:TILES * width], a[:, step * width:TILES * width],
                                      a[:, 0:(TILES - step) * width], ALU.add))
        a, b, step = b, a, 2 * step
    return a


def choose(core, t, free):
    nc = core.nc
    w = Work(core, free)
    u, hits, ties, total, scan, bad = (w.sb(f"ch_{k}", [P, TILES], F32) for k in ("u", "hits", "ties", "total", "scan", "bad"))
    count, rank, sign, bit_f, need = (w.sb(f"ch_{k}", [P, 1], F32) for k in ("count", "rank", "sign", "bit_f", "need"))
    bits, cand, keep, bit = (w.sb(f"ch_{k}", [P, 1], I32) for k in ("bits", "cand", "keep", "bit"))
    link, counted, summed, loop_link, bit_link = core.sems("ch_link", "ch_counted", "ch_summed", "ch_loop_link", "ch_bit_link")
    ROUNDS = 31
    ps = core.bank[0]
    with nc.Block() as block:

        @block.vector
        def _(dve):
            chain = Chain(dve, link)

            def everywhere(n):
                dve.sem_inc(counted, 1)
                dve.wait_ge(summed, n)

            chain(nc.vector.tensor_scalar(bad[:, :], t["valid"][:, :], -1.0, -FAR, ALU.add, ALU.mult))
            chain(nc.vector.tensor_scalar(hits[:, :], t["router"][:, :], 0.0, None, ALU.is_ge))
            chain(nc.vector.tensor_tensor(hits[:, :], hits[:, :], t["valid"][:, :], ALU.mult))
            chain(nc.vector.tensor_reduce(count[:, :], hits[:, :], AX.X, ALU.add))
            everywhere(1)
            chain(nc.vector.tensor_scalar(rank[:, :], ps[:, 0:1], float(CHOSEN), None, ALU.is_lt))
            chain(nc.vector.tensor_scalar(sign[:, :], rank[:, :], -2.0, 1.0, ALU.mult, ALU.add))
            chain(nc.vector.tensor_scalar(rank[:, :], rank[:, :], float(NODES + 1 - 2 * CHOSEN), float(CHOSEN), ALU.mult, ALU.add))
            chain(nc.vector.tensor_scalar(u[:, :], t["router"][:, :], sign[:, :], None, ALU.mult))
            chain(nc.vector.tensor_tensor(u[:, :], u[:, :], t["valid"][:, :], ALU.mult))
            chain(nc.vector.tensor_tensor(u[:, :], u[:, :], bad[:, :], ALU.add))
            chain(nc.vector.memset(bits[:, :], 0))
            chain(nc.vector.memset(bit_f[:, :], 2.0 ** (ROUNDS - 1)))
            chain(nc.vector.tensor_copy(bit[:, :], bit_f[:, :]))
            PER = 5
            with dve.Fori(0, ROUNDS) as r:
                dve.wait_ge(loop_link, r * PER)
                nc.vector.tensor_tensor(cand[:, :], bits[:, :], bit[:, :], ALU.bitwise_or).then_inc(loop_link, 1)
                dve.wait_ge(loop_link, r * PER + 1)
                nc.vector.tensor_scalar(hits[:, :], u[:, :], cand[:, :].bitcast(F32), None, ALU.is_ge).then_inc(loop_link, 1)
                dve.wait_ge(loop_link, r * PER + 2)
                nc.vector.tensor_reduce(count[:, :], hits[:, :], AX.X, ALU.add).then_inc(counted, 1)
                dve.wait_ge(summed, r + 2)
                nc.vector.scalar_tensor_tensor(out=keep[:, :], in0=ps[:, 0:1], scalar=rank[:, :], in1=bit_f[:, :],
                                               op0=ALU.is_ge, op1=ALU.mult).then_inc(loop_link, 1)
                dve.wait_ge(loop_link, r * PER + 3)
                nc.vector.tensor_tensor(bits[:, :], bits[:, :], keep[:, :], ALU.bitwise_or).then_inc(loop_link, 1)
                nc.vector.tensor_scalar(bit_f[:, :], bit_f[:, :], 0.5, None, ALU.mult).then_inc(bit_link, 1)
                dve.wait_ge(bit_link, r + 1)
                nc.vector.tensor_copy(bit[:, :], bit_f[:, :]).then_inc(loop_link, 1)
            dve.wait_ge(loop_link, ROUNDS * PER)
            chain(nc.vector.tensor_scalar(sign[:, :], sign[:, :], bits[:, :].bitcast(F32), None, ALU.mult))
            chain(nc.vector.tensor_scalar(ties[:, :], t["router"][:, :], sign[:, :], None, ALU.is_equal))
            chain(nc.vector.tensor_tensor(ties[:, :], ties[:, :], t["valid"][:, :], ALU.mult))
            chain(nc.vector.tensor_scalar(hits[:, :], t["router"][:, :], sign[:, :], None, ALU.is_gt))
            chain(nc.vector.tensor_tensor(hits[:, :], hits[:, :], t["valid"][:, :], ALU.mult))
            chain(nc.vector.tensor_reduce(count[:, :], hits[:, :], AX.X, ALU.add))
            everywhere(ROUNDS + 2)
            chain(nc.vector.tensor_scalar(need[:, :], ps[:, 0:1], -1.0, float(CHOSEN), ALU.mult, ALU.add))
            chain(nc.vector.tensor_copy(total[:, :], core.bank[1][:, 0:TILES]))
            run = scan_tiles(chain, nc, total, scan, 1)
            chain(nc.vector.tensor_tensor(run[:, :], run[:, :], core.bank[1][:, 0:TILES], ALU.subtract))
            chain(nc.vector.tensor_tensor(run[:, :], run[:, :], core.bank[2][:, 0:TILES], ALU.add))
            chain(nc.vector.tensor_scalar(run[:, :], run[:, :], need[:, :], None, ALU.is_lt))
            chain(nc.vector.tensor_tensor(ties[:, :], ties[:, :], run[:, :], ALU.mult))
            chain(nc.vector.tensor_tensor(hits[:, :], hits[:, :], ties[:, :], ALU.add))
            chain(nc.vector.tensor_tensor(t["chosen"][:, :], hits[:, :], t["router"][:, :], ALU.mult))

        @block.tensor
        def _(pe):
            pe.wait_ge(counted, 1)
            pe.matmul(ps[:, 0:1], t["ones"][:, :], count[:, :], start=True, stop=True).then_inc(summed, 1)
            with pe.Fori(0, ROUNDS) as r:
                pe.wait_ge(counted, r + 2)
                pe.matmul(ps[:, 0:1], t["ones"][:, :], count[:, :], start=True, stop=True).then_inc(summed, 1)
            pe.wait_ge(counted, ROUNDS + 2)
            pe.matmul(core.bank[1][:, 0:TILES], t["ones"][:, :], ties[:, :], start=True, stop=True)
            pe.matmul(core.bank[2][:, 0:TILES], t["before"][:, :], ties[:, :], start=True, stop=True)
            pe.matmul(ps[:, 0:1], t["ones"][:, :], count[:, :], start=True, stop=True).then_inc(summed, 1)


def table1(core, t, dram, free, wrel, wgate):
    nc = core.nc
    w = Work(core, free)
    pair = lambda name, cols, dt: [w.sb(f"t1_{name}{b}", [P, cols], dt) for b in range(2)]
    xn, xhi, xlo = pair("xn", D, F32), pair("xhi", D, F16), pair("xlo", D, F16)
    raw, gate, row = pair("raw", RELS, F32), pair("gate", RELS, F32), pair("row", RELS * 2 * D, F16)
    norm_done, turned, xhi_done, xlo_done, logit_done, raw_done, gate_done, rel_done, hi_done, lo_done = core.sems(
        "t1_norm_done", "t1_turned", "t1_xhi_done", "t1_xlo_done", "t1_logit_done", "t1_raw_done", "t1_gate_done", "t1_rel_done",
        "t1_hi_done", "t1_lo_done")
    stored = core.sems("t1_stored0", "t1_stored1")
    psT, psG, psR = core.bank[0:2], core.bank[2:4], core.bank[4:8]
    DEPTH = 2
    PAIRS = RELS // 2
    tab = dram["table1"].rearrange("(n r) d -> n (r d)", r=RELS)

    def slots(eng, slot):
        with eng.Fori(0, TILES // 2 - 1) as i:
            for b in range(2):
                slot(2 * i + b, b, 2)
        slot(TILES - 2, 0, 1)
        slot(TILES - 1, 1, 0)

    with nc.Block() as block:

        @block.sync
        def _(sp):
            for b in range(2):
                sp.sem_inc(stored[b], 16)
            with sp.Fori(0, TILES // 2) as i:
                for b in range(2):
                    n = 2 * i + b
                    sp.wait_ge(lo_done, (n + 1 + DEPTH) * RELS)
                    sp.dma_start(tab[bass.ds(n * P, P), :], row[b][:, :]).then_inc(stored[b], 16)
            for b in range(2):
                sp.wait_ge(stored[b], 16 * (TILES // 2) + 16)

        @block.vector
        def _(dve):
            for s, n in ((norm_done, DEPTH), (xlo_done, DEPTH), (gate_done, DEPTH), (lo_done, DEPTH * RELS)):
                dve.sem_inc(s, n)

            def norm(n, b):
                dve.wait_ge(turned, n + 1)
                normed(nc, xn[b][:, :], t["acc"], n, t["mean"], t["rstd"]).then_inc(norm_done, 1)

            def xlow(n, b):
                dve.wait_ge(xhi_done, n + 1 + DEPTH)
                nc.vector.scalar_tensor_tensor(out=xlo[b][:, :], in0=psT[b][:, 0:D], scalar=X_SCALE, in1=xhi[b][:, :],
                                               op0=ALU.mult, op1=ALU.subtract).then_inc(xlo_done, 1)

            def scale_gate(n, b):
                dve.wait_ge(lo_done, (n - 1 + DEPTH) * RELS)
                dve.wait_ge(raw_done, n + 1 + DEPTH)
                nc.vector.tensor_scalar(gate[b][:, :], raw[b][:, :], MSG_SCALE / (X_SCALE * W_SCALE), None, ALU.mult).then_inc(gate_done, 1)

            def low(n, b, r):
                if r % 2 == 0:
                    dve.wait_ge(hi_done, (n + DEPTH) * RELS + r + 2)
                at = psR[r // 2 % 4][:, (r % 2) * D:(r % 2 + 1) * D]
                hi, lo = (row[b][:, (2 * r + j) * D:(2 * r + j + 1) * D] for j in range(2))
                nc.vector.scalar_tensor_tensor(out=lo, in0=at, scalar=gate[b][:, r:r + 1], in1=hi,
                                               op0=ALU.mult, op1=ALU.subtract).then_inc(lo_done, 1)

            def slot(n, b, more):
                if more > 1:
                    norm(n + 2, b)
                if more:
                    xlow(n + 1, 1 - b)
                for r in range(RELS):
                    low(n, b, r)
                    if r == RELS // 2 + 1 and more:
                        scale_gate(n + 1, 1 - b)

            norm(0, 0)
            norm(1, 1)
            xlow(0, 0)
            scale_gate(0, 0)
            slots(dve, slot)

        @block.scalar
        def _(act):
            for s, n in ((xhi_done, DEPTH), (raw_done, DEPTH), (hi_done, DEPTH * RELS)):
                act.sem_inc(s, n)

            def xhigh(n, b):
                core.hold(act, "act", rel_done, (n - 1 + DEPTH) * PAIRS)
                core.hold(act, "act", turned, n + 1 + DEPTH)
                nc.scalar.activation(xhi[b][:, :], psT[b][:, 0:D], ACT.Copy, scale=X_SCALE).then_inc(xhi_done, 1)

            def sigmoid(n, b):
                core.hold(act, "act", gate_done, n + 1)
                core.hold(act, "act", logit_done, n + 1 + DEPTH)
                nc.scalar.activation(raw[b][:, :], psG[b][:, 0:RELS], ACT.Sigmoid, scale=1.0 / (X_SCALE * W_SCALE)).then_inc(raw_done, 1)

            def high(n, b, r):
                if r == 0:
                    core.hold(act, "act", gate_done, n + 1 + DEPTH)
                    core.hold(act, "act", stored[b], (n - b) * 8 + 16)
                if r % 2 == 0:
                    core.hold(act, "act", rel_done, (n + DEPTH) * PAIRS + r // 2 + 1)
                at = psR[r // 2 % 4][:, (r % 2) * D:(r % 2 + 1) * D]
                nc.scalar.activation(row[b][:, 2 * r * D:(2 * r + 1) * D], at, ACT.Copy, scale=gate[b][:, r:r + 1]).then_inc(hi_done, 1)

            def slot(n, b, more):
                if more:
                    xhigh(n + 1, 1 - b)
                for r in range(RELS):
                    high(n, b, r)
                    if r == RELS // 2 - 1 and more:
                        sigmoid(n + 1, 1 - b)

            xhigh(0, 0)
            sigmoid(0, 0)
            slots(act, slot)

        @block.tensor
        def _(pe):
            for s, n in ((turned, DEPTH), (logit_done, DEPTH), (rel_done, DEPTH * PAIRS)):
                pe.sem_inc(s, n)

            def turn(n, b):
                pe.wait_ge(xlo_done, n + 1)
                pe.wait_ge(norm_done, n + 1 + DEPTH)
                for c in range(KC):
                    last = pe.transpose(psT[b][:, c * P:(c + 1) * P], xn[b][:, c * P:(c + 1) * P], t["ident"][:, :])
                last.then_inc(turned, 1)

            def product(out, b, right):
                for k in range(KC):
                    hi, lo = xhi[b][:, k * P:(k + 1) * P], xlo[b][:, k * P:(k + 1) * P]
                    rhi, rlo = right(0, k), right(1, k)
                    nc.tensor.matmul(out, hi, rhi, start=k == 0, stop=False)
                    nc.tensor.matmul(out, hi, rlo, start=False, stop=False)
                    last = nc.tensor.matmul(out, lo, rhi, start=False, stop=k == KC - 1)
                return last

            def logits(n, b):
                pe.wait_ge(raw_done, n + 1)
                pe.wait_ge(xlo_done, n + 1 + DEPTH)
                product(psG[b][:, 0:RELS], b, lambda j, k: wgate[j][:, k * RELS:(k + 1) * RELS]).then_inc(logit_done, 1)

            def relations(n, b, q):
                pe.wait_ge(lo_done, (n + DEPTH) * RELS + 2 * (q + 1 - 4))
                at = lambda j, k: wrel[j][:, (k * RELS + 2 * q) * D:(k * RELS + 2 * q + 2) * D]
                product(psR[q % 4][:, :], b, at).then_inc(rel_done, 1)

            def slot(n, b, more):
                if more:
                    turn(n + 1, 1 - b)
                for q in range(PAIRS):
                    relations(n, b, q)
                    if q == PAIRS // 2 - 1 and more:
                        logits(n + 1, 1 - b)

            turn(0, 0)
            logits(0, 0)
            slots(pe, slot)


def score(core, t, dram, free, logits):
    nc = core.nc
    w = Work(core, free)
    xn = [w.sb(f"sc_xn{b}", [P, 2 * D], F32) for b in range(2)]
    xT = [w.sb(f"sc_xT{b}", [P, 2 * D], F32) for b in range(2)]
    row = [w.sb(f"sc_row{b}", [P, 2 * 2 * D], F16) for b in range(2)]
    wg = w.sb("sc_wg", [P, KC * EXPERTS], F32)
    loaded, norm_done, turned, xT_done, mm_done, out_done, hi_done, lo_done, x_stored = core.sems(
        "sc_loaded", "sc_norm_done", "sc_turned", "sc_xT_done", "sc_mm_done", "sc_out_done", "sc_hi_done", "sc_lo_done", "x_stored")
    stored = core.sems("sc_stored0", "sc_stored1")
    psT, psL = core.bank[0:2], core.bank[2:4]
    DEPTH = 2
    N = TILES // 2
    rows = dram["rows"].rearrange("(n p) d -> p n d", p=P)

    def slots(eng, slot):
        body = (N - 2) // 2
        with eng.Fori(0, body) as i:
            for b in range(2):
                slot(2 * i + b, b, N)
        for n in range(2 * body, N):
            slot(n, n % 2, N - n)

    halves = lambda b, j: row[b][:, :].rearrange("p (n j d) -> p n j d", j=2, d=D)[:, :, j, :]
    both = lambda x: x[:, :].rearrange("p (n d) -> p n d", d=D)
    with nc.Block() as block:

        @block.sync
        def _(sp):
            for b in range(2):
                sp.sem_inc(stored[b], 16)
            sp.dma_start(wg[:, :].rearrange("p (c e) -> p c e", c=KC), dram["wg"].rearrange("(c p) e -> p c e", p=P)).then_inc(loaded, 16)
            sp.dma_start(dram["x3"].rearrange("(n p) d -> p n d", p=P), t["acc"][:, :].rearrange("p (n d) -> p n d", d=D)).then_inc(x_stored, 16)

            def store(n, b, left):
                sp.wait_ge(lo_done, n + 1 + DEPTH)
                at = rows[:, 2 * n:2 * n + 2, :] if isinstance(n, int) else rows[:, bass.ds(2 * n, 2), :]
                sp.dma_start(at, row[b][:, :].rearrange("p (n d) -> p n d", n=2)).then_inc(stored[b], 16)

            slots(sp, store)
            sp.wait_ge(x_stored, 16)
            for b in range(2):
                sp.wait_ge(stored[b], 16 * ((N + 1 - b) // 2) + 16)

        @block.vector
        def _(dve):
            for s in (norm_done, out_done, lo_done):
                dve.sem_inc(s, DEPTH)

            def norm(n, b):
                dve.wait_ge(turned, n + 1)
                dve.wait_ge(lo_done, n + 1)
                for k in range(2):
                    last = normed(nc, xn[b][:, k * D:(k + 1) * D], t["acc"], 2 * n + k, t["mean"], t["rstd"])
                last.then_inc(norm_done, 1)

            def low(n, b):
                dve.wait_ge(hi_done, n + 1 + DEPTH)
                nc.vector.scalar_tensor_tensor(out=halves(b, 1), in0=both(xn[b]), scalar=X_SCALE, in1=halves(b, 0),
                                               op0=ALU.mult, op1=ALU.subtract).then_inc(lo_done, 1)

            def result(n, b):
                dve.wait_ge(mm_done, n + 1 + DEPTH)
                for k in range(2):
                    last = nc.vector.tensor_tensor(tile_of(logits, 2 * n + k, EXPERTS), psL[b][:, k * EXPERTS:(k + 1) * EXPERTS], t["bg"][:, :], ALU.add)
                last.then_inc(out_done, 1)

            def slot(n, b, left):
                low(n, b)
                if left > 2:
                    norm(n + 2, b)
                result(n, b)

            for b in range(2):
                norm(b, b)
            slots(dve, slot)

        @block.scalar
        def _(act):
            act.sem_inc(hi_done, DEPTH)
            act.sem_inc(xT_done, DEPTH)

            def slot(n, b, left):
                core.hold(act, "act", stored[b], (n - b) * 8 + 16)
                core.hold(act, "act", norm_done, n + 1 + DEPTH)
                nc.scalar.activation(halves(b, 0), both(xn[b]), ACT.Copy, scale=X_SCALE).then_inc(hi_done, 1)
                core.hold(act, "act", mm_done, n + 1)
                core.hold(act, "act", turned, n + 1 + DEPTH)
                nc.scalar.activation(xT[b][:, :], psT[b][:, :], ACT.Copy).then_inc(xT_done, 1)

            slots(act, slot)

        @block.tensor
        def _(pe):
            pe.sem_inc(turned, DEPTH)
            pe.sem_inc(mm_done, DEPTH)
            pe.wait_ge(loaded, 16)

            def turn(n, b):
                pe.wait_ge(xT_done, n + 1)
                pe.wait_ge(norm_done, n + 1 + DEPTH)
                for c in range(2 * KC):
                    last = pe.transpose(psT[b][:, c * P:(c + 1) * P], xn[b][:, c * P:(c + 1) * P], t["ident"][:, :])
                last.then_inc(turned, 1)

            def product(n, b):
                pe.wait_ge(out_done, n + 1)
                pe.wait_ge(xT_done, n + 1 + DEPTH)
                for k in range(2):
                    for c in range(KC):
                        last = pe.matmul(psL[b][:, k * EXPERTS:(k + 1) * EXPERTS], xT[b][:, (k * KC + c) * P:(k * KC + c + 1) * P],
                                         wg[:, c * EXPERTS:(c + 1) * EXPERTS], start=c == 0, stop=c == KC - 1)
                last.then_inc(mm_done, 1)

            def slot(n, b, left):
                if left > 1:
                    turn(n + 1, 1 - b)
                product(n, b)

            turn(0, 0)
            slots(pe, slot)


def place(core, t, free, logits, places):
    nc = core.nc
    w = Work(core, free)
    wide = [w.sb(f"pl_wide{k}", [P, TILES * EXPERTS * EXPERTS], F32) for k in range(2)]
    rank, picked, total, scan, masked = (w.sb(f"pl_{k}", [P, TILES * EXPERTS], F32) for k in ("rank", "picked", "total", "scan", "masked"))
    best = [w.sb(f"pl_best{k}", [P, TILES], F32) for k in range(TOP)]
    pos = w.sb("pl_pos", [P, TILES], F32)
    part_i = w.sb("pl_part_i", [P, TILES], I32)
    spot = lambda f, k: places[f][:, :].rearrange("p (n k) -> p n k", k=TOP)[:, :, k]
    one = w.sb("pl_one", [P, TILES], F32)
    count, full, start = (w.sb(f"pl_{k}", [P, EXPERTS], F32) for k in ("count", "full", "start"))
    full_i = w.sb("pl_full_i", [P, EXPERTS], I32)
    tile_no = w.sb("pl_tile_no", [1, PLACE_TILES], F32)
    over = w.sb("pl_over", [1, PLACE_TILES * EXPERTS], F32)
    owner = w.sb("pl_owner", [1, PLACE_TILES], F32)
    earlier = w.sb("pl_earlier", [P, EXPERTS * EXPERTS], F32)
    link, numbered, picks_ready, exped, exp_ready, summed = core.sems(
        "pl_link", "pl_numbered", "pl_picks_ready", "pl_exped", "pl_exp_ready", "pl_summed")
    psB, psT = core.bank[0], core.bank[1]
    TE = TILES * EXPERTS
    with nc.Block() as block:

        @block.gpsimd
        def _(pool):
            pool.iota(tile_no[:, :], pattern=[[TOKENS, PLACE_TILES]], base=0, channel_multiplier=0,
                      allow_small_or_imprecise_dtypes=True).then_inc(numbered, 1)

        @block.vector
        def _(dve):
            chain = Chain(dve, link)
            l3 = logits[:, :].rearrange("p (n e) -> p n e", e=EXPERTS)
            w4 = [x[:, :].rearrange("p (n e j) -> p n e j", e=EXPERTS, j=EXPERTS) for x in wide]
            shape = [P, TILES, EXPERTS, EXPERTS]
            of_j, of_e = l3.unsqueeze(2).to_broadcast(shape), l3.unsqueeze(3).to_broadcast(shape)
            r3 = rank[:, :].rearrange("p (n e) -> p n e", e=EXPERTS)
            e2 = earlier[:, :].rearrange("p (e j) -> p e j", j=EXPERTS)
            chain(nc.vector.memset(earlier[:, :], 0.0))
            for e in range(1, EXPERTS):
                chain(nc.vector.memset(earlier[:, e * EXPERTS:e * EXPERTS + e], 1.0))
            chain(nc.vector.tensor_tensor(w4[0], of_j, of_e, ALU.is_equal))
            chain(nc.vector.tensor_tensor(w4[0], w4[0], e2.unsqueeze(1).to_broadcast(shape), ALU.mult))
            chain(nc.vector.tensor_tensor(w4[1], of_j, of_e, ALU.is_gt))
            chain(nc.vector.tensor_tensor(wide[0][:, :], wide[0][:, :], wide[1][:, :], ALU.add))
            chain(nc.vector.tensor_reduce(r3, w4[0], AX.X, ALU.add))
            chain(nc.vector.tensor_scalar(picked[:, :], rank[:, :], float(TOP), None, ALU.is_lt))
            p3 = picked[:, :].rearrange("p (n e) -> p n e", e=EXPERTS)
            chain(nc.vector.tensor_tensor(p3, p3, t["valid"][:, :].unsqueeze(2).to_broadcast([P, TILES, EXPERTS]), ALU.mult))
            dve.sem_inc(picks_ready, 1)
            m3 = masked[:, :].rearrange("p (n e) -> p n e", e=EXPERTS)
            for k in range(TOP):
                chain(nc.vector.tensor_scalar(masked[:, :], rank[:, :], float(k), None, ALU.is_equal))
                chain(nc.vector.tensor_tensor(masked[:, :], masked[:, :], logits[:, :], ALU.mult))
                chain(nc.vector.tensor_reduce(best[k][:, :], m3, AX.X, ALU.add))
            chain(nc.vector.tensor_tensor(best[1][:, :], best[1][:, :], best[0][:, :], ALU.subtract))
            dve.sem_inc(exp_ready, 1)
            dve.wait_ge(exped, 1)
            chain(nc.vector.tensor_scalar(pos[:, :], one[:, :], 1.0, None, ALU.add))
            chain(nc.vector.reciprocal(t["share0"][:, :], pos[:, :]))
            chain(nc.vector.tensor_tensor(t["share1"][:, :], t["share0"][:, :], one[:, :], ALU.mult))
            dve.wait_ge(summed, 1)
            chain(nc.vector.tensor_copy(total[:, :], psT[:, 0:TE]))
            run = scan_tiles(chain, nc, total, scan, EXPERTS)
            chain(nc.vector.tensor_copy(count[:, :], run[:, TE - EXPERTS:TE]))
            chain(nc.vector.tensor_tensor(run[:, :], run[:, :], psT[:, 0:TE], ALU.subtract))
            chain(nc.vector.tensor_tensor(run[:, :], run[:, :], psB[:, 0:TE], ALU.add))
            chain(nc.vector.tensor_scalar(full[:, :], count[:, :], float(TOKENS - 1), None, ALU.add))
            chain(nc.vector.tensor_copy(full_i[:, :], full[:, :]))
            chain(nc.vector.tensor_scalar(full_i[:, :], full_i[:, :], ~(TOKENS - 1), None, ALU.bitwise_and))
            chain(nc.vector.tensor_copy(full[:, :], full_i[:, :]))
            chain(nc.vector.memset(start[:, :], 0.0))
            for e in range(1, EXPERTS):
                chain(nc.vector.tensor_tensor(start[:, e:e + 1], start[:, e - 1:e], full[:, e - 1:e], ALU.add))
            run3 = run[:, :].rearrange("p (n e) -> p n e", e=EXPERTS)
            chain(nc.vector.tensor_tensor(run3, run3, start[:, :].unsqueeze(1).to_broadcast([P, TILES, EXPERTS]), ALU.add))
            for k in range(TOP):
                chain(nc.vector.tensor_scalar(masked[:, :], rank[:, :], float(k), None, ALU.is_equal))
                chain(nc.vector.tensor_tensor(masked[:, :], masked[:, :], run[:, :], ALU.mult))
                chain(nc.vector.tensor_reduce(pos[:, :], m3, AX.X, ALU.add))
                chain(nc.vector.tensor_tensor(pos[:, :], pos[:, :], t["valid"][:, :], ALU.mult))
                chain(nc.vector.tensor_copy(t[f"take{k}"][:, :], pos[:, :]))
                for f, (op, by) in enumerate(((ALU.arith_shift_right, P.bit_length() - 1), (ALU.bitwise_and, P - 1))):
                    chain(nc.vector.tensor_scalar(part_i[:, :], t[f"take{k}"][:, :], by, None, op))
                    chain(nc.vector.tensor_copy(pos[:, :], part_i[:, :]))
                    chain(nc.vector.scalar_tensor_tensor(out=pos[:, :], in0=pos[:, :], scalar=1.0, in1=t["valid"][:, :],
                                                         op0=ALU.add, op1=ALU.mult))
                    chain(nc.vector.tensor_scalar(spot(f, k), pos[:, :], -1.0, None, ALU.add))
            chain(nc.vector.tensor_tensor(start[:, :], start[:, :], full[:, :], ALU.add))
            dve.wait_ge(numbered, 1)
            over3 = over[:, :].rearrange("p (n e) -> p n e", e=EXPERTS)
            shape = [1, PLACE_TILES, EXPERTS]
            chain(nc.vector.tensor_tensor(over3, start[0:1, :].unsqueeze(1).to_broadcast(shape),
                                          tile_no[:, :].unsqueeze(2).to_broadcast(shape), ALU.is_le))
            chain(nc.vector.tensor_reduce(owner[:, :], over3, AX.X, ALU.add))
            chain(nc.vector.tensor_scalar(owner[:, :], owner[:, :], float(EXPERTS - 1), None, ALU.min))
            chain(nc.vector.tensor_copy(t["owner"][:, :], owner[:, :]))

        @block.scalar
        def _(act):
            act.wait_ge(exp_ready, 1)
            nc.scalar.activation(one[:, :], best[1][:, :], ACT.Exp).then_inc(exped, 1)

        @block.tensor
        def _(pe):
            pe.wait_ge(picks_ready, 1)
            pe.matmul(psB[:, 0:TE], t["before"][:, :], picked[:, :], start=True, stop=True)
            pe.matmul(psT[:, 0:TE], t["ones"][:, :], picked[:, :], start=True, stop=True).then_inc(summed, 1)


def invert(core, t, free, places):
    nc = core.nc
    w = Work(core, free)
    PICKS = GROUP * TOP
    pair = lambda name, cols, dt: [w.sb(f"in_{name}{b}", [P, cols], dt) for b in range(2)]
    hot_row, hot_tile = pair("hot_row", PICKS * P, F16), pair("hot_tile", PICKS * PLACE_COLS, F16)
    parts = pair("parts", PICKS * 2 * PLACE_COLS, F16)
    numbers = pair("numbers", GROUP, F32)
    zeros = w.sb("in_zeros", [P, 2 * PLACE_COLS], F16)
    node = w.sb("in_node", [P, PLACE_COLS], F32)
    node_no = w.sb("in_node_no", [P, TILES], F32)
    numbered, row_done, tile_done, number_done, parts_done, mm_done, summed, link = core.sems(*(
        f"in_{k}" for k in ("numbered", "row_done", "tile_done", "number_done", "parts_done", "mm_done", "summed", "link")))
    ps = core.bank[0][:, 0:2 * PLACE_COLS]
    DEPTH = 2
    groups = TILES // GROUP
    tile_pick, row_pick = places
    with nc.Block() as block:

        @block.gpsimd
        def _(pool):
            pool.iota(node_no[:, :], pattern=[[1, TILES]], base=1, channel_multiplier=0, allow_small_or_imprecise_dtypes=True).then_inc(numbered, 1)
            pool.memset(zeros[:, :], 0.0).then_inc(numbered, 1)

        @block.vector
        def _(dve):
            dve.sem_inc(tile_done, DEPTH)
            with dve.Fori(0, groups // 2) as i:
                for b in range(2):
                    n = 2 * i + b
                    core.hold(dve, "dve", mm_done, n + 1)
                    core.hold(dve, "dve", parts_done, n + 1)
                    for hot, width, pick, done in ((hot_row[b], P, row_pick, row_done), (hot_tile[b], PLACE_COLS, tile_pick, tile_done)):
                        shape = [P, PICKS, width]
                        nc.vector.tensor_tensor(hot[:, :].rearrange("p (s q) -> p s q", q=width),
                                                t["iota16"][:, 0:width].unsqueeze(1).to_broadcast(shape),
                                                pick[:, bass.ds(n * PICKS, PICKS)].unsqueeze(2).to_broadcast(shape), ALU.is_equal).then_inc(done, 1)
            dve.wait_ge(summed, 1)
            chain = Chain(dve, link)
            chain(nc.vector.tensor_scalar(node[:, :], ps[:, 0:PLACE_COLS], float(P), float(-P), ALU.mult, ALU.add))
            chain(nc.vector.tensor_tensor(node[:, :], node[:, :], ps[:, PLACE_COLS:2 * PLACE_COLS], ALU.add))
            chain(nc.vector.tensor_scalar(node[:, :], node[:, :], 0.0, None, ALU.max))
            chain(nc.vector.tensor_copy(t["node_at"][:, :], node[:, :]))

        @block.scalar
        def _(act):
            act.sem_inc(parts_done, DEPTH)
            act.wait_ge(numbered, 2)
            with act.Fori(0, groups // 2) as i:
                for b in range(2):
                    n = 2 * i + b
                    hot = hot_tile[b][:, :].rearrange("p (s q) -> p s q", q=PLACE_COLS)
                    part = parts[b][:, :].rearrange("p (s j q) -> p s j q", j=2, q=PLACE_COLS)
                    core.hold(act, "act", mm_done, n + 1)
                    core.hold(act, "act", tile_done, n + 1 + DEPTH)
                    nc.scalar.activation(numbers[b][:, :], node_no[:, bass.ds(n * GROUP, GROUP)], ACT.Copy).then_inc(number_done, 1)
                    nc.scalar.activation(part[:, :, 1, :], hot, ACT.Copy, scale=t["part"][:, 0:1])
                    core.hold(act, "act", number_done, n + 1)
                    for k in range(GROUP):
                        cut = slice(k * TOP, (k + 1) * TOP)
                        last = nc.scalar.activation(part[:, cut, 0, :], hot[:, cut, :], ACT.Copy, scale=numbers[b][:, k:k + 1])
                    last.then_inc(parts_done, 1)

        @block.tensor
        def _(pe):
            pe.sem_inc(mm_done, DEPTH)
            pe.wait_ge(numbered, 2)
            pe.matmul(ps, t["ident16"][:, :], zeros[:, :], start=True, stop=False)
            with pe.Fori(0, groups // 2) as i:
                for b in range(2):
                    n = 2 * i + b
                    pe.wait_ge(row_done, n + 1)
                    pe.wait_ge(parts_done, n + 1 + DEPTH)
                    for k in range(PICKS):
                        last = pe.matmul(ps, hot_row[b][:, k * P:(k + 1) * P], parts[b][:, k * 2 * PLACE_COLS:(k + 1) * 2 * PLACE_COLS],
                                         start=False, stop=False)
                    last.then_inc(mm_done, 1)
            pe.matmul(ps, t["ident16"][:, :], zeros[:, :], start=False, stop=True).then_inc(summed, 1)


def experts(core, t, dram, free, w1, w2, b1, b2):
    nc = core.nc
    w = Work(core, free)
    pair = lambda name, cols, dt: [w.sb(f"ex_{name}{b}", [P, cols], dt) for b in range(2)]
    xin, xT = pair("xin", SUBS * 2 * D, F16), pair("xT", 2 * KC * TOKENS, F16)
    g, ghi, glo = w.sb("ex_g", [P, HC * TOKENS], F32), w.sb("ex_ghi", [P, HC * TOKENS], F16), w.sb("ex_glo", [P, HC * TOKENS], F16)
    sum_, y, idx = pair("sum", D, F32), pair("y", SUBS * D, F32), pair("idx", SUBS, I32)
    idx_done, turned, xT_done, up_done, gelu_done, ghi_done, glo_done, down_done, sum_done, y_done = core.sems(*(
        f"ex_{k}" for k in ("idx_done", "turned", "xT_done", "up_done", "gelu_done", "ghi_done", "glo_done", "down_done", "sum_done", "y_done")))
    x_in, y_out = core.sems("ex_x_in0", "ex_x_in1"), core.sems("ex_y_out0", "ex_y_out1")
    psT, psH, psY = core.bank[0:2], core.bank[2:6], core.bank[6:8]
    BANKS = len(psH)
    DEPTH = 2
    N = PLACE_TILES
    results = dram["results"].rearrange("(n s p) d -> n p s d", s=SUBS, p=P)

    def slots(eng, slot):
        with eng.Fori(0, N // 2 - 1) as i:
            for b in range(2):
                slot(2 * i + b, b, N)
        slot(N - 2, 0, 2)
        slot(N - 1, 1, 1)

    def owner(eng, n):
        at = t["owner"][0:1, n:n + 1] if isinstance(n, int) else t["owner"][0:1, bass.ds(n, 1)]
        return eng.value_load(at, min_val=0, max_val=EXPERTS - 1)

    with nc.Block() as block:

        @block.gpsimd
        def _(pool):
            pool.sem_inc(idx_done, DEPTH)
            with pool.Fori(0, N // 2) as i:
                for b in range(2):
                    n = 2 * i + b
                    core.hold(pool, "pool", turned, n + 1)
                    pool.tensor_copy(idx[b][:, :], t["node_at"][:, bass.ds(n * SUBS, SUBS)]).then_inc(idx_done, 1)
                    core.hold(pool, "pool", idx_done, n + 1 + DEPTH)
                    for s in range(SUBS):
                        pool.indirect_dma_start(out=xin[b][:, s * 2 * D:(s + 1) * 2 * D], out_offset=None, in_=dram["rows"],
                                                in_offset=bass.IndirectOffsetOnAxis(ap=idx[b][:, s:s + 1], axis=0)).then_inc(x_in[b], 16)

        @block.sync
        def _(sp):
            for b in range(2):
                sp.sem_inc(y_out[b], 16)
            def store(n, b, left):
                sp.wait_ge(y_done, SUBS * (n + 1 + DEPTH))
                at = results[n:n + 1] if isinstance(n, int) else results[bass.ds(n, 1)]
                sp.dma_start(at.rearrange("n p s d -> p (n s) d"), y[b][:, :].rearrange("p (s d) -> p s d", d=D)).then_inc(y_out[b], 16)

            slots(sp, store)
            for b in range(2):
                sp.wait_ge(y_out[b], 16 * (N // 2) + 16)

        @block.vector
        def _(dve):
            dve.sem_inc(glo_done, 1)
            dve.sem_inc(ghi_done, 1)
            dve.sem_inc(sum_done, SUBS * DEPTH)
            dve.sem_inc(y_done, SUBS * DEPTH)

            def split(n):
                dve.wait_ge(gelu_done, BANKS * (n + 2))
                core.hold(dve, "dve", down_done, SUBS * (n + 1))
                nc.vector.tensor_scalar(ghi[:, :], g[:, :], H_SCALE, None, ALU.mult).then_inc(ghi_done, 1)
                dve.wait_ge(ghi_done, n + 2)
                nc.vector.scalar_tensor_tensor(out=glo[:, :], in0=g[:, :], scalar=H_SCALE, in1=ghi[:, :],
                                               op0=ALU.mult, op1=ALU.subtract).then_inc(glo_done, 1)

            def result(n, b):
                e = owner(dve, n)
                core.hold(dve, "dve", y_out[b], (n - b) * 8 + 16)
                bias = b2[:, bass.ds(e * D, D)]
                for s in range(SUBS):
                    core.hold(dve, "dve", down_done, SUBS * (n + 1) + s + 1)
                    nc.vector.scalar_tensor_tensor(out=sum_[s][:, :], in0=psY[s][:, 0:D], scalar=1.0 / (H_SCALE * W_SCALE), in1=bias,
                                                   op0=ALU.mult, op1=ALU.add).then_inc(sum_done, 1)
                for s in range(SUBS):
                    dve.wait_ge(sum_done, SUBS * (n + DEPTH) + s + 1)
                    nc.vector.scalar_tensor_tensor(out=y[b][:, s * D:(s + 1) * D], in0=psY[s][:, D:2 * D], scalar=1.0 / (H_SCALE * W_SCALE),
                                                   in1=sum_[s][:, :], op0=ALU.mult, op1=ALU.add).then_inc(y_done, 1)

            def slot(n, b, left):
                if left > 1:
                    split(n + 1)
                result(n, b)

            split(0)
            slots(dve, slot)

        @block.scalar
        def _(act):
            act.sem_inc(xT_done, DEPTH)
            act.sem_inc(gelu_done, BANKS)

            def copy(n, b):
                core.hold(act, "act", up_done, BANKS * (n + 1))
                core.hold(act, "act", turned, n + 1 + DEPTH)
                nc.scalar.activation(xT[b][:, :], psT[b][:, :].bitcast(F16), ACT.Copy).then_inc(xT_done, 1)

            def gelu(n):
                e = owner(act, n)
                core.hold(act, "act", glo_done, n + 1)
                for j in range(BANKS):
                    core.hold(act, "act", up_done, BANKS * (n + DEPTH) + j + 1)
                    for c in (2 * j, 2 * j + 1):
                        last = nc.scalar.activation(g[:, c * TOKENS:(c + 1) * TOKENS], psH[j][:, (c % 2) * TOKENS:(c % 2 + 1) * TOKENS],
                                                    ACT.Gelu, bias=b1[:, bass.ds(e * HC + c, 1)], scale=1.0 / (X_SCALE * W_SCALE))
                    last.then_inc(gelu_done, 1)

            def slot(n, b, left):
                if left > 1:
                    gelu(n + 1)
                if left > 2:
                    copy(n + 2, b)

            copy(0, 0)
            gelu(0)
            copy(1, 1)
            slots(act, slot)

        @block.tensor
        def _(pe):
            pe.sem_inc(turned, DEPTH)
            pe.sem_inc(up_done, BANKS * DEPTH)
            pe.sem_inc(down_done, SUBS)

            def turn(n, b):
                pe.wait_ge(xT_done, n + 1)
                pe.wait_ge(x_in[b], (n - b) * 8 * SUBS + 16 * SUBS)
                ps = psT[b][:, :].bitcast(F16)
                for s in range(SUBS):
                    for c in range(2 * KC):
                        last = pe.transpose(ps[:, c * TOKENS + s * P:c * TOKENS + (s + 1) * P],
                                            xin[b][:, (s * 2 * KC + c) * P:(s * 2 * KC + c + 1) * P], t["ident16"][:, :])
                last.then_inc(turned, 1)

            def up(n, b):
                e = owner(pe, n)
                pe.wait_ge(xT_done, n + 1 + DEPTH)
                for j in range(BANKS):
                    pe.wait_ge(gelu_done, BANKS * n + j + 1)
                    for c in (2 * j, 2 * j + 1):
                        out = psH[j][:, (c % 2) * TOKENS:(c % 2 + 1) * TOKENS]
                        for k in range(KC):
                            at = (k * HC + c) * 2 * P
                            whi, wlo = (w1[:, bass.ds(e * KC * H * 2 + (at + h * P), P)] for h in range(2))
                            hi, lo = (xT[b][:, (h * KC + k) * TOKENS:(h * KC + k + 1) * TOKENS] for h in range(2))
                            pe.matmul(out, whi, hi, start=k == 0, stop=False)
                            pe.matmul(out, whi, lo, start=False, stop=False)
                            last = pe.matmul(out, wlo, hi, start=False, stop=k == KC - 1)
                    last.then_inc(up_done, 1)

            def down(n, b):
                e = owner(pe, n)
                pe.wait_ge(y_done, SUBS * (n - 1 + DEPTH) + SUBS)
                pe.wait_ge(glo_done, n + 2)
                for c in range(HC):
                    at = e * HC * D * 2 + c * 2 * D
                    both, whi = w2[:, bass.ds(at, 2 * D)], w2[:, bass.ds(at, D)]
                    for s in range(SUBS):
                        hi, lo = (x[:, c * TOKENS + s * P:c * TOKENS + (s + 1) * P] for x in (ghi, glo))
                        if c < HC - 1:
                            pe.matmul(psY[s][:, :], hi, both, start=c == 0, stop=False)
                            pe.matmul(psY[s][:, 0:D], lo, whi, start=False, stop=False)
                        else:
                            pe.matmul(psY[s][:, 0:D], lo, whi, start=False, stop=False)
                            pe.matmul(psY[s][:, :], hi, both, start=False, stop=True).then_inc(down_done, 1)

            def slot(n, b, left):
                if left > 2:
                    turn(n + 2, b)
                if left > 1:
                    up(n + 1, 1 - b)
                down(n, b)

            for n in range(2):
                turn(n, n)
            up(0, 0)
            slots(pe, slot)


def combine(core, t, dram, free, out):
    nc = core.nc
    w = Work(core, free)
    pair = lambda name, cols, dt: [w.sb(f"co_{name}{b}", [P, cols], dt) for b in range(2)]
    x3, half, done, take = pair("x3", D, F32), pair("half", D, F32), pair("done", D, F32), pair("take", TOP, I32)
    y = [pair(f"y{k}_", D, F32) for k in range(TOP)]
    idx_done, half_done, sum_done = core.sems("co_idx_done", "co_half_done", "co_sum_done")
    x_in, y_in, stored = core.sems("co_x_in0", "co_x_in1"), core.sems("co_y_in0", "co_y_in1"), core.sems("co_stored0", "co_stored1")
    DEPTH = 2
    with nc.Block() as block:

        @block.gpsimd
        def _(pool):
            with pool.Fori(0, TILES // 2) as i:
                for b in range(2):
                    n = 2 * i + b
                    core.hold(pool, "pool", sum_done, n + 1)
                    for k in range(TOP):
                        pool.tensor_copy(take[b][:, k:k + 1], col(t[f"take{k}"], n)).then_inc(idx_done, 1)
                    core.hold(pool, "pool", idx_done, TOP * (n + 1))
                    for k in range(TOP):
                        pool.indirect_dma_start(out=y[k][b][:, :], out_offset=None, in_=dram["results"],
                                                in_offset=bass.IndirectOffsetOnAxis(ap=take[b][:, k:k + 1], axis=0)).then_inc(y_in[b], 16)

        @block.sync
        def _(sp):
            with sp.Fori(0, TILES // 2) as i:
                for b in range(2):
                    n = 2 * i + b
                    sp.wait_ge(sum_done, n + 1)
                    sp.dma_start(x3[b][:, :], dram["x3"][bass.ds(n * P, P), :]).then_inc(x_in[b], 16)

        @block.vector
        def _(dve):
            dve.sem_inc(sum_done, DEPTH)
            dve.sem_inc(half_done, DEPTH)
            with dve.Fori(0, TILES // 2) as i:
                for b in range(2):
                    n = 2 * i + b
                    dve.wait_ge(sum_done, n + 1)
                    dve.wait_ge(x_in[b], 16 * (i + 1))
                    dve.wait_ge(y_in[b], 16 * TOP * (i + 1))
                    core.hold(dve, "dve", stored[b], 16 * i + 16)
                    nc.vector.scalar_tensor_tensor(out=half[b][:, :], in0=y[0][b][:, :], scalar=col(t["share0"], n), in1=x3[b][:, :],
                                                   op0=ALU.mult, op1=ALU.add).then_inc(half_done, 1)
                    dve.wait_ge(half_done, n + 1 + DEPTH)
                    nc.vector.scalar_tensor_tensor(out=done[b][:, :], in0=y[1][b][:, :], scalar=col(t["share1"], n), in1=half[b][:, :],
                                                   op0=ALU.mult, op1=ALU.add).then_inc(sum_done, 1)

        @block.scalar
        def _(act):
            for b in range(2):
                act.sem_inc(stored[b], 16)
            with act.Fori(0, TILES // 2) as i:
                for b in range(2):
                    n = 2 * i + b
                    core.hold(act, "act", sum_done, n + 1 + DEPTH)
                    act.dma_start(out[bass.ds(n * P, P), :], done[b][:, :]).then_inc(stored[b], 16)
            for b in range(2):
                act.wait_ge(stored[b], 16 * (TILES // 2) + 16)


def load_biases(core, dram, b1, b2):
    loaded = core.sem("biases_loaded")
    with core.nc.Block() as block:

        @block.sync
        def _(sp):
            sp.dma_start(b1[:, :], dram["b1_1"]).then_inc(loaded, 16)
            sp.dma_start(b2[:, :], dram["b2_1"].partition_broadcast(P)).then_inc(loaded, 16)
            sp.wait_ge(loaded, 32)


def program(nc, dram, out):
    with ExitStack() as ctx:
        core = Core(nc, ctx)
        t = {}
        for name, shape, dt in (
            ("ident", [P, P], F32), ("before", [P, P], F32), ("ones", [P, P], F32), ("ident16", [P, P], F16),
            ("iota16", [P, P], F16), ("part", [P, STEP_CHUNKS], F32), ("valid", [P, TILES], F32),
            ("b0", [P, D], F32), ("wr", [P, D], F32), ("b2_0", [P, D], F32), ("br", [P, 1], F32), ("bg", [P, EXPERTS], F32),
            ("b1_0", [P, HC], F32), ("stats", [P, TILES * 6], F32),
            ("mean", [P, TILES], F32), ("rstd", [P, TILES], F32), ("router", [P, TILES], F32), ("chosen", [P, TILES], F32),
            ("share0", [P, TILES], F32), ("share1", [P, TILES], F32), ("owner", [1, PLACE_TILES], I32),
            ("take0", [P, TILES], I32), ("take1", [P, TILES], I32), ("node_at", [P, PLACE_COLS], I32),
        ):
            t[name] = core.sb(name, shape, dt)
        core.ln_tmp = [core.sb(f"ln_{k}", [P, TILES], F32) for k in ("half", "var", "tmp")]
        experts_free = core.at
        for name, shape, dt in (
            ("acc", [P, TILES * D], F32), ("side", [P, TILES * D], F32),
            ("idx1", [P, STEP_COLS], I32), ("step_cols", [P, STEP_COLS * COLS], F32), ("win", [1, STEP_COLS], I32),
            ("last_step", [1, WINDOWS], I32),
        ):
            t[name] = core.sb(name, shape, dt)
        free = core.at
        for name, shape, dt in (("idx0", [P, STEP_COLS], I32),):
            t[name] = core.sb(name, shape, dt)
        first_free = core.at
        prepare(core, t, dram)
        moments(core, "ln0", t["acc"], t["stats"], t["mean"], t["rstd"])
        table0(core, t, dram, first_free)
        gather(core, t, dram["table0"], 0, t["side"], first_free)
        w = Work(core, free)
        w1 = [w.sb(f"w1_0_{h}", [P, KC * H], F16) for h in ("hi", "lo")]
        w2 = [w.sb(f"w2_0_{h}", [P, HC * D], F16) for h in ("hi", "lo")]
        s = Work(core, w.at)
        stage = [s.sb(f"stage_0_{k}", [P, 2 * H], F32) for k in range(2)]
        split_weights(core, [
            (dram["w1_0"].rearrange("(c p) h -> p c h", p=P), *[stage[0][:, :].rearrange("p (c h) -> p c h", c=KC)] * 2,
             w1[0][:, :].rearrange("p (c h) -> p c h", c=KC), w1[1][:, :].rearrange("p (c h) -> p c h", c=KC), None),
            (dram["w2_0"].rearrange("(c p) d -> p c d", p=P), *[stage[1][:, :].rearrange("p (c d) -> p c d", c=HC)] * 2,
             w2[0][:, :].rearrange("p (c d) -> p c d", c=HC), w2[1][:, :].rearrange("p (c d) -> p c d", c=HC), None),
        ], W_SCALE, "split0")

        def take_sum(dve, i):
            at = tile_of(t["acc"], i, GROUP * D)
            return nc.vector.scalar_tensor_tensor(out=at, in0=tile_of(t["side"], i, GROUP * D), scalar=1.0, in1=at,
                                                  op0=ALU.mult, op1=ALU.add)

        moments(core, "ln1", t["acc"], t["stats"], t["mean"], t["rstd"], first=take_sum)
        ffn0(core, t, w.at, w1, w2)
        choose(core, t, free)

        w = Work(core, free)
        wrel = [w.sb(f"wrel_{h}", [P, KC * RELS * D], F16) for h in ("hi", "lo")]
        wgate = [w.sb(f"wgate_{h}", [P, KC * RELS], F16) for h in ("hi", "lo")]
        s = Work(core, w.at)
        gate_stage = s.sb("stage_gate", [P, KC * RELS], F32)
        stage = [s.sb(f"stage_1_{k}", [P, RELS * D], F32) for k in range(KC)]
        loads = [(dram["wgate"].rearrange("(c p) r -> p c r", p=P), *[gate_stage[:, :].rearrange("p (c r) -> p c r", c=KC)] * 2,
                  wgate[0][:, :].rearrange("p (c r) -> p c r", c=KC), wgate[1][:, :].rearrange("p (c r) -> p c r", c=KC), None)]
        for c in range(KC):
            cut = slice(c * RELS * D, (c + 1) * RELS * D)
            loads.append((dram["wrel"][:, c * P:(c + 1) * P, :].rearrange("r p o -> p r o"), *[stage[c][:, :].rearrange("p (r o) -> p r o", o=D)] * 2,
                          wrel[0][:, cut].rearrange("p (r o) -> p r o", o=D), wrel[1][:, cut].rearrange("p (r o) -> p r o", o=D), None))
        split_weights(core, loads, W_SCALE, "split1")

        def take_ffn(dve, i):
            for k in range(GROUP):
                n = i * GROUP + k
                last = nc.vector.scalar_tensor_tensor(out=tile_of(t["acc"], n), in0=tile_of(t["side"], n), scalar=col(t["chosen"], n),
                                                      in1=tile_of(t["acc"], n), op0=ALU.mult, op1=ALU.add)
            return last

        moments(core, "ln2", t["acc"], t["stats"], t["mean"], t["rstd"], first=take_ffn)
        table1(core, t, dram, w.at, wrel, wgate)
        gather(core, t, dram["table1"], 1, t["side"], free)

        def take_gnn(dve, i):
            at = tile_of(t["acc"], i, GROUP * D)
            return nc.vector.scalar_tensor_tensor(out=at, in0=tile_of(t["side"], i, GROUP * D), scalar=0.0, in1=at,
                                                  op0=ALU.max, op1=ALU.add)

        moments(core, "ln3", t["acc"], t["stats"], t["mean"], t["rstd"], first=take_gnn)
        w = Work(core, free)
        logits = w.sb("logits", [P, TILES * EXPERTS], F32)
        score(core, t, dram, w.at, logits)
        places = [w.sb(f"place_{k}", [P, TILES * TOP], F16) for k in ("tile", "row")]
        place(core, t, w.at, logits, places)
        invert(core, t, w.at, places)

        w = Work(core, experts_free)
        w1 = w.sb("w1_1", [P, EXPERTS * KC * H * 2], F16)
        w2 = w.sb("w2_1", [P, EXPERTS * HC * D * 2], F16)
        b1 = w.sb("b1_1", [P, EXPERTS * HC], F32)
        b2 = w.sb("b2_1", [P, EXPERTS * D], F32)
        s = Work(core, w.at)
        stage = [s.sb(f"stage_2_{k}", [P, 2 * H], F32) for k in range(STAGES)]
        loads = []
        for e in range(EXPERTS):
            for view, c, both, width in ((dram["w1_1"][e].rearrange("(c p) h -> p c h", p=P), KC, w1, P),
                                         (dram["w2_1"][e].rearrange("(c p) d -> p c d", p=P), HC, w2, D)):
                k = len(loads)
                stage_k = stage[k % STAGES]
                half = lambda j: both[:, e * 4 * H:(e + 1) * 4 * H].rearrange("p (c j d) -> p c j d", j=2, d=width)[:, :, j, :]
                loads.append((view, stage_k[:, :].rearrange("p (c h) -> p c h", c=c), stage_k[:, :].rearrange("p (c d) -> p c d", d=width),
                              half(0), half(1), k - STAGES if k >= STAGES else None))
        split_weights(core, loads, W_SCALE, "split2")
        load_biases(core, dram, b1, b2)
        experts(core, t, dram, w.at, w1, w2, b1, b2)
        combine(core, t, dram, w.at, out)


def kernel(x, src, dst, edge_type_16, edge_weight, edge_weight1, L0_gnn_W, L0_gnn_b, L0_ffn_attention_mask, L0_ffn_wr, L0_ffn_br,
           L0_ffn_w1, L0_ffn_b1, L0_ffn_w2, L0_ffn_b2, L1_gnn_weight, L1_gnn_gate_weight, L1_ffn_Wg, L1_ffn_bg, L1_ffn_W1,
           L1_ffn_b1, L1_ffn_W2, L1_ffn_b2):
    import concourse.bacc as _bacc
    from concourse.bass_utils import run_bass_kernel_spmd as _run

    def edge_tiles(a, fill):
        a = np.asarray(a).reshape(-1)
        return np.pad(a, (0, EDGE_ROWS * P - EDGES), constant_values=fill).reshape(EDGE_ROWS, P)

    f = np.asarray
    far = WINDOWS * P
    dst_tiles = edge_tiles(dst, far)
    edges = np.concatenate([edge_tiles(src, 0), dst_tiles, edge_tiles(edge_type_16, 0),
                            edge_tiles(edge_weight, 0).view(np.int32), edge_tiles(edge_weight1, 0).view(np.int32)], axis=1)
    node = np.arange(TILES)[None, :] * P + np.arange(P)[:, None]
    arrays = {
        "x": np.pad(f(x), ((0, ROWS - NODES), (0, 0))),
        "edges": edges, "dst_last": dst_tiles[:, P - 1].reshape(1, EDGE_ROWS),
        "ident": np.eye(P, dtype=np.float32), "before": np.triu(np.ones((P, P), np.float32), 1),
        "valid": (node < NODES).astype(np.float32),
        "w0T": f(L0_gnn_W).T, "b0": f(L0_gnn_b).reshape(1, D),
        "wr": f(L0_ffn_wr).reshape(1, D), "br": f(L0_ffn_br).reshape(1, 1),
        "w1_0": f(L0_ffn_w1), "b1_0": f(L0_ffn_b1).reshape(HC, P).T, "w2_0": f(L0_ffn_w2), "b2_0": f(L0_ffn_b2).reshape(1, D),
        "wrel": f(L1_gnn_weight), "wgate": f(L1_gnn_gate_weight).reshape(RELS, D).T,
        "wg": f(L1_ffn_Wg), "bg": f(L1_ffn_bg).reshape(1, EXPERTS),
        "w1_1": f(L1_ffn_W1), "b1_1": f(L1_ffn_b1).reshape(EXPERTS * HC, P).T,
        "w2_1": f(L1_ffn_W2), "b2_1": f(L1_ffn_b2).reshape(1, EXPERTS * D),
    }
    arrays = {k: np.ascontiguousarray(v) for k, v in arrays.items()}
    nc = _bacc.Bacc("TRN2", target_bir_lowering=False, num_devices=1)
    dram = {k: nc.dram_tensor(f"in_{k}", v.shape, mybir.dt.from_np(v.dtype), kind="ExternalInput").ap() for k, v in arrays.items()}
    dram["table0"] = nc.dram_tensor("table0", (ROWS, 2 * D), F16, kind="Internal").ap()
    dram["table1"] = nc.dram_tensor("table1", (ROWS * RELS, 2 * D), F16, kind="Internal").ap()
    dram["rows"] = nc.dram_tensor("rows", (ROWS, 2 * D), F16, kind="Internal").ap()
    dram["results"] = nc.dram_tensor("results", (PLACES, D), F32, kind="Internal").ap()
    dram["x3"] = nc.dram_tensor("x3", (ROWS, D), F32, kind="Internal").ap()
    out = nc.dram_tensor("out", (ROWS, D), F32, kind="ExternalOutput").ap()
    program(nc, dram, out)
    r = _run(nc, [{f"in_{k}": v for k, v in arrays.items()}], core_ids=[0])
    return r.results[0]["out"][:NODES]
```
